# Optimizing a Trainium2 kernel written in Bass

```python
import numpy as np
import jax
import jax.numpy as jnp

def _softmax(x, axis=-1):
    return jax.nn.softmax(x, axis=axis)

def _gelu(x):
    return jax.nn.gelu(x, approximate=True)

def _silu(x):
    return jax.nn.silu(x)

def _sigmoid(x):
    return jax.nn.sigmoid(x)

def _layernorm(x, axis=-1, eps=1e-05):
    m = jnp.mean(x, axis=axis, keepdims=True)
    v = jnp.var(x, axis=axis, keepdims=True)
    return (x - m) / jnp.sqrt(v + eps)

def _scatter_add(tgt, idx, src, axis=0):
    return tgt.at[idx].add(src)

def _segment_sum(src, seg, n):
    return jax.ops.segment_sum(src, seg, n)
kernel_name = 'mk_hybrid_d1_jaxref_r8_f778f1'

def setup_inputs(seed: int=0):
    np.random.seed(seed)
    _w = jnp.asarray

    def _L0_attn_a_setup():
        import jax, jax.numpy as jnp
        import numpy as np
        DIM, H, P, N = (256, 32, 64, 128)
        K = 4

        def _causal_conv(u, w):
            T = u.shape[1]
            up = jnp.pad(u, ((0, 0), (K - 1, 0), (0, 0), (0, 0)))
            out = jnp.zeros_like(u)
            for k in range(K):
                out = out + up[:, k:k + T] * w[:, :, k]
            return out
        key = jax.random.key(seed)
        ks = jax.random.split(key, 8)
        proj_dim = 2 * H * P + 2 * H * N + H
        x = jax.random.normal(ks[0], (2, 256, DIM), dtype=jnp.float32)
        Win = jax.random.normal(ks[1], (proj_dim, DIM), dtype=jnp.float32) * 0.02
        Wout = jax.random.normal(ks[2], (DIM, H * P), dtype=jnp.float32) * 0.02
        A_log = jnp.linspace(-3.0, -1.0, H, dtype=jnp.float32)
        dt_bias = jnp.zeros((H,), dtype=jnp.float32)
        conv_w_x = jax.random.normal(ks[3], (H, P, K), dtype=jnp.float32) * 0.1
        conv_w_b = jax.random.normal(ks[4], (H, N, K), dtype=jnp.float32) * 0.1
        conv_w_c = jax.random.normal(ks[5], (H, N, K), dtype=jnp.float32) * 0.1
        return {'x': x, 'Win': Win, 'Wout': Wout, 'A_log': A_log, 'dt_bias': dt_bias, 'conv_w_x': conv_w_x, 'conv_w_b': conv_w_b, 'conv_w_c': conv_w_c}
    _L0_attn_a_in = _L0_attn_a_setup()

    def _L0_attn_b_setup():
        import jax, jax.numpy as jnp
        import numpy as np
        from jax import lax
        BATCH = 2
        SEQ = 256
        HID = 256
        EXPAND = 2
        INTER = EXPAND * HID
        HEADS = 64
        PDIM = INTER // HEADS
        NSTATE = 128
        G = 1
        HPG = HEADS // G
        KCONV = 4
        GTS = G * NSTATE
        CONV_DIM = INTER + 2 * GTS
        PROJ_DIM = 2 * INTER + 2 * GTS + HEADS
        EPS = 1e-05
        MUP = (0.25, 0.5, 0.5, 0.5, 1.0)

        def _mup_vector():
            return jnp.concatenate([jnp.full((INTER,), MUP[0], jnp.float32), jnp.full((INTER,), MUP[1], jnp.float32), jnp.full((GTS,), MUP[2], jnp.float32), jnp.full((GTS,), MUP[3], jnp.float32), jnp.full((HEADS,), MUP[4], jnp.float32)])

        def _forward(hidden_states, in_proj_w, conv_w, conv_b, A_log, D, dt_bias, norm_w, out_proj_w):
            b, l, _ = hidden_states.shape
            proj = hidden_states @ in_proj_w * _mup_vector()
            z = proj[..., :INTER]
            xBC = proj[..., INTER:INTER + CONV_DIM]
            dt = proj[..., INTER + CONV_DIM:]
            xBC_cl = jnp.swapaxes(xBC, 1, 2)
            conv = lax.conv_general_dilated(xBC_cl, conv_w[:, None, :], window_strides=(1,), padding=((KCONV - 1, 0),), feature_group_count=CONV_DIM)
            xBC = jax.nn.silu(jnp.swapaxes(conv + conv_b[None, :, None], 1, 2))
            x = xBC[..., :INTER].reshape(b, l, G, HPG, PDIM)
            Bm = xBC[..., INTER:INTER + GTS].reshape(b, l, G, NSTATE)
            Cm = xBC[..., INTER + GTS:].reshape(b, l, G, NSTATE)
            dt = jax.nn.softplus(dt + dt_bias)
            A = -jnp.exp(A_log)
            dA = jnp.exp(dt * A).reshape(b, l, G, HPG)
            dtx = dt.reshape(b, l, G, HPG)[..., None] * x

            def step(state, inp):
                dA_t, dtx_t, B_t, C_t = inp
                state = state * dA_t[..., None, None] + jnp.einsum('bgcp,bgn->bgcpn', dtx_t, B_t)
                y_t = jnp.einsum('bgn,bgcpn->bgcp', C_t, state)
                return (state, y_t)
            inputs = (jnp.moveaxis(dA, 1, 0), jnp.moveaxis(dtx, 1, 0), jnp.moveaxis(Bm, 1, 0), jnp.moveaxis(Cm, 1, 0))
            state0 = jnp.zeros((b, G, HPG, PDIM, NSTATE), hidden_states.dtype)
            _, ys = lax.scan(step, state0, inputs)
            y = jnp.moveaxis(ys, 0, 1) + D.reshape(1, 1, G, HPG, 1) * x
            y = y.reshape(b, l, INTER)
            yg = y.reshape(b, l, G, INTER // G)
            var = jnp.mean(jnp.square(yg), axis=-1, keepdims=True)
            yn = (yg * lax.rsqrt(var + EPS)).reshape(b, l, INTER) * norm_w
            out = yn * jax.nn.silu(z)
            return out @ out_proj_w
        key = jax.random.key(seed)
        ks = jax.random.split(key, 8)
        hidden_states = jax.random.normal(ks[0], (BATCH, SEQ, HID), jnp.float32)
        in_proj_w = jax.random.normal(ks[1], (HID, PROJ_DIM), jnp.float32) * 0.02
        conv_w = jax.random.normal(ks[2], (CONV_DIM, KCONV), jnp.float32) * 0.2
        conv_b = jnp.zeros((CONV_DIM,), jnp.float32)
        A_log = jnp.log(jnp.arange(1, HEADS + 1, dtype=jnp.float32))
        D = jnp.ones((HEADS,), jnp.float32)
        dt_bias = jax.random.uniform(ks[3], (HEADS,), jnp.float32)
        norm_w = jnp.ones((INTER,), jnp.float32)
        out_proj_w = jax.random.normal(ks[4], (INTER, HID), jnp.float32) * 0.02
        return dict(hidden_states=hidden_states, in_proj_w=in_proj_w, conv_w=conv_w, conv_b=conv_b, A_log=A_log, D=D, dt_bias=dt_bias, norm_w=norm_w, out_proj_w=out_proj_w)
    _L0_attn_b_in = _L0_attn_b_setup()

    def _L0_ffn_setup():
        import jax, jax.numpy as jnp
        import numpy as np
        B, S, D, F, E, SH, K = (2, 256, 256, 128, 16, 2, 2)

        def _experts_all(x, g, gb, w1, b1, w2, b2):
            y = jax.nn.gelu(jnp.einsum('bsd,edf->bsef', x, g) + gb, approximate=False)
            y = y * (jnp.einsum('bsd,edf->bsef', x, w1) + b1)
            return jnp.einsum('bsef,efd->bsed', y, w2) + b2
        key = jax.random.key(seed)
        ks = jax.random.split(key, 8)
        std = 0.02
        mk = lambda k, sh: jax.random.normal(k, sh, jnp.float32) * std
        return {'x': jax.random.normal(ks[0], (B, S, D), jnp.float32), 'wa': mk(ks[1], (D, E)), 'rg': mk(ks[2], (E, D, F)), 'rgb': jnp.zeros((E, F), jnp.float32), 'rw1': mk(ks[3], (E, D, F)), 'rb1': jnp.zeros((E, F), jnp.float32), 'rw2': mk(ks[4], (E, F, D)), 'rb2': jnp.zeros((E, D), jnp.float32), 'sg': mk(ks[5], (SH, D, F)), 'sgb': jnp.zeros((SH, F), jnp.float32), 'sw1': mk(ks[6], (SH, D, F)), 'sb1': jnp.zeros((SH, F), jnp.float32), 'sw2': mk(ks[7], (SH, F, D)), 'sb2': jnp.zeros((SH, D), jnp.float32)}
    _L0_ffn_in = _L0_ffn_setup()
    _d = {'L0_attn_a_x': _L0_attn_a_in['x'], 'L0_attn_a_Win': _L0_attn_a_in['Win'], 'L0_attn_a_Wout': _L0_attn_a_in['Wout'], 'L0_attn_a_A_log': _L0_attn_a_in['A_log'], 'L0_attn_a_dt_bias': _L0_attn_a_in['dt_bias'], 'L0_attn_a_conv_w_x': _L0_attn_a_in['conv_w_x'], 'L0_attn_a_conv_w_b': _L0_attn_a_in['conv_w_b'], 'L0_attn_a_conv_w_c': _L0_attn_a_in['conv_w_c'], 'L0_attn_b_in_proj_w': _L0_attn_b_in['in_proj_w'], 'L0_attn_b_conv_w': _L0_attn_b_in['conv_w'], 'L0_attn_b_conv_b': _L0_attn_b_in['conv_b'], 'L0_attn_b_A_log': _L0_attn_b_in['A_log'], 'L0_attn_b_D': _L0_attn_b_in['D'], 'L0_attn_b_dt_bias': _L0_attn_b_in['dt_bias'], 'L0_attn_b_norm_w': _L0_attn_b_in['norm_w'], 'L0_attn_b_out_proj_w': _L0_attn_b_in['out_proj_w'], 'L0_ffn_wa': _L0_ffn_in['wa'], 'L0_ffn_rg': _L0_ffn_in['rg'], 'L0_ffn_rgb': _L0_ffn_in['rgb'], 'L0_ffn_rw1': _L0_ffn_in['rw1'], 'L0_ffn_rb1': _L0_ffn_in['rb1'], 'L0_ffn_rw2': _L0_ffn_in['rw2'], 'L0_ffn_rb2': _L0_ffn_in['rb2'], 'L0_ffn_sg': _L0_ffn_in['sg'], 'L0_ffn_sgb': _L0_ffn_in['sgb'], 'L0_ffn_sw1': _L0_ffn_in['sw1'], 'L0_ffn_sb1': _L0_ffn_in['sb1'], 'L0_ffn_sw2': _L0_ffn_in['sw2'], 'L0_ffn_sb2': _L0_ffn_in['sb2']}
    _x0 = _d['L0_attn_a_x']
    _d['L0_attn_a_x'] = jax.random.normal(jax.random.fold_in(jax.random.key(seed), 1), (1, 1024, 256), dtype=_x0.dtype)
    del _x0
    return _d

def reference(L0_attn_a_x, L0_attn_a_Win, L0_attn_a_Wout, L0_attn_a_A_log, L0_attn_a_dt_bias, L0_attn_a_conv_w_x, L0_attn_a_conv_w_b, L0_attn_a_conv_w_c, L0_attn_b_in_proj_w, L0_attn_b_conv_w, L0_attn_b_conv_b, L0_attn_b_A_log, L0_attn_b_D, L0_attn_b_dt_bias, L0_attn_b_norm_w, L0_attn_b_out_proj_w, L0_ffn_wa, L0_ffn_rg, L0_ffn_rgb, L0_ffn_rw1, L0_ffn_rb1, L0_ffn_rw2, L0_ffn_rb2, L0_ffn_sg, L0_ffn_sgb, L0_ffn_sw1, L0_ffn_sb1, L0_ffn_sw2, L0_ffn_sb2):

    def _L0_attn_a_ref(x, Win, Wout, A_log, dt_bias, conv_w_x, conv_w_b, conv_w_c):
        import jax, jax.numpy as jnp
        import numpy as np
        DIM, H, P, N = (256, 32, 64, 128)
        K = 4

        def _causal_conv(u, w):
            T = u.shape[1]
            up = jnp.pad(u, ((0, 0), (K - 1, 0), (0, 0), (0, 0)))
            out = jnp.zeros_like(u)
            for k in range(K):
                out = out + up[:, k:k + T] * w[:, :, k]
            return out
        B, T, _ = x.shape
        proj = x @ Win.T
        x_ssm = proj[..., :H * P].reshape(B, T, H, P)
        z = proj[..., H * P:2 * H * P].reshape(B, T, H, P)
        Bm = proj[..., 2 * H * P:2 * H * P + H * N].reshape(B, T, H, N)
        Cm = proj[..., 2 * H * P + H * N:2 * H * P + 2 * H * N].reshape(B, T, H, N)
        dt_raw = proj[..., 2 * H * P + 2 * H * N:]
        dt = jax.nn.softplus(dt_raw + dt_bias)
        xc = jax.nn.silu(_causal_conv(x_ssm, conv_w_x))
        Bc = jax.nn.silu(_causal_conv(Bm, conv_w_b))
        Cc = jax.nn.silu(_causal_conv(Cm, conv_w_c))
        A = -jnp.exp(A_log)
        decay = jnp.exp(dt * A)
        dtx = dt[..., None] * xc

        def step(h, inp):
            dec_t, dtx_t, B_t, C_t = inp
            h = dec_t[..., None, None] * h + dtx_t[..., None] * B_t[:, :, None, :]
            y = jnp.einsum('bhpn,bhn->bhp', h, C_t)
            return (h, y)
        h0 = jnp.zeros((B, H, P, N), dtype=x.dtype)
        xs = (jnp.moveaxis(decay, 1, 0), jnp.moveaxis(dtx, 1, 0), jnp.moveaxis(Bc, 1, 0), jnp.moveaxis(Cc, 1, 0))
        _, ys = jax.lax.scan(step, h0, xs)
        y = jnp.moveaxis(ys, 0, 1)
        y = y * jax.lax.rsqrt(jnp.mean(y * y, axis=-1, keepdims=True) + 1e-06)
        y = y * jax.nn.silu(z)
        return y.reshape(B, T, H * P) @ Wout.T

    def _L0_attn_b_ref(hidden_states, in_proj_w, conv_w, conv_b, A_log, D, dt_bias, norm_w, out_proj_w):
        import jax, jax.numpy as jnp
        import numpy as np
        from jax import lax
        BATCH = 2
        SEQ = 256
        HID = 256
        EXPAND = 2
        INTER = EXPAND * HID
        HEADS = 64
        PDIM = INTER // HEADS
        NSTATE = 128
        G = 1
        HPG = HEADS // G
        KCONV = 4
        GTS = G * NSTATE
        CONV_DIM = INTER + 2 * GTS
        PROJ_DIM = 2 * INTER + 2 * GTS + HEADS
        EPS = 1e-05
        MUP = (0.25, 0.5, 0.5, 0.5, 1.0)

        def _mup_vector():
            return jnp.concatenate([jnp.full((INTER,), MUP[0], jnp.float32), jnp.full((INTER,), MUP[1], jnp.float32), jnp.full((GTS,), MUP[2], jnp.float32), jnp.full((GTS,), MUP[3], jnp.float32), jnp.full((HEADS,), MUP[4], jnp.float32)])

        def _forward(hidden_states, in_proj_w, conv_w, conv_b, A_log, D, dt_bias, norm_w, out_proj_w):
            b, l, _ = hidden_states.shape
            proj = hidden_states @ in_proj_w * _mup_vector()
            z = proj[..., :INTER]
            xBC = proj[..., INTER:INTER + CONV_DIM]
            dt = proj[..., INTER + CONV_DIM:]
            xBC_cl = jnp.swapaxes(xBC, 1, 2)
            conv = lax.conv_general_dilated(xBC_cl, conv_w[:, None, :], window_strides=(1,), padding=((KCONV - 1, 0),), feature_group_count=CONV_DIM)
            xBC = jax.nn.silu(jnp.swapaxes(conv + conv_b[None, :, None], 1, 2))
            x = xBC[..., :INTER].reshape(b, l, G, HPG, PDIM)
            Bm = xBC[..., INTER:INTER + GTS].reshape(b, l, G, NSTATE)
            Cm = xBC[..., INTER + GTS:].reshape(b, l, G, NSTATE)
            dt = jax.nn.softplus(dt + dt_bias)
            A = -jnp.exp(A_log)
            dA = jnp.exp(dt * A).reshape(b, l, G, HPG)
            dtx = dt.reshape(b, l, G, HPG)[..., None] * x

            def step(state, inp):
                dA_t, dtx_t, B_t, C_t = inp
                state = state * dA_t[..., None, None] + jnp.einsum('bgcp,bgn->bgcpn', dtx_t, B_t)
                y_t = jnp.einsum('bgn,bgcpn->bgcp', C_t, state)
                return (state, y_t)
            inputs = (jnp.moveaxis(dA, 1, 0), jnp.moveaxis(dtx, 1, 0), jnp.moveaxis(Bm, 1, 0), jnp.moveaxis(Cm, 1, 0))
            state0 = jnp.zeros((b, G, HPG, PDIM, NSTATE), hidden_states.dtype)
            _, ys = lax.scan(step, state0, inputs)
            y = jnp.moveaxis(ys, 0, 1) + D.reshape(1, 1, G, HPG, 1) * x
            y = y.reshape(b, l, INTER)
            yg = y.reshape(b, l, G, INTER // G)
            var = jnp.mean(jnp.square(yg), axis=-1, keepdims=True)
            yn = (yg * lax.rsqrt(var + EPS)).reshape(b, l, INTER) * norm_w
            out = yn * jax.nn.silu(z)
            return out @ out_proj_w
        return _forward(hidden_states, in_proj_w, conv_w, conv_b, A_log, D, dt_bias, norm_w, out_proj_w)

    def _L0_ffn_ref(x, wa, rg, rgb, rw1, rb1, rw2, rb2, sg, sgb, sw1, sb1, sw2, sb2):
        import jax, jax.numpy as jnp
        import numpy as np
        B, S, D, F, E, SH, K = (2, 256, 256, 128, 16, 2, 2)

        def _experts_all(x, g, gb, w1, b1, w2, b2):
            y = jax.nn.gelu(jnp.einsum('bsd,edf->bsef', x, g) + gb, approximate=False)
            y = y * (jnp.einsum('bsd,edf->bsef', x, w1) + b1)
            return jnp.einsum('bsef,efd->bsed', y, w2) + b2
        aff = jax.nn.sigmoid(jnp.einsum('bsd,de->bse', x, wa))
        topk_p, topk_i = jax.lax.top_k(aff, K)
        topk_p = topk_p / jnp.sum(topk_p, axis=-1, keepdims=True)
        combine = jnp.sum(jax.nn.one_hot(topk_i, E, dtype=x.dtype) * topk_p[..., None], axis=2)
        routed = jnp.einsum('bsed,bse->bsd', _experts_all(x, rg, rgb, rw1, rb1, rw2, rb2), combine)
        shared = jnp.sum(_experts_all(x, sg, sgb, sw1, sb1, sw2, sb2), axis=2)
        return x + shared + routed
    x = L0_attn_a_x
    x = x + _L0_attn_a_ref(_layernorm(x, axis=-1), L0_attn_a_Win, L0_attn_a_Wout, L0_attn_a_A_log, L0_attn_a_dt_bias, L0_attn_a_conv_w_x, L0_attn_a_conv_w_b, L0_attn_a_conv_w_c)
    x = x + _L0_ffn_ref(_layernorm(x, axis=-1), L0_ffn_wa, L0_ffn_rg, L0_ffn_rgb, L0_ffn_rw1, L0_ffn_rb1, L0_ffn_rw2, L0_ffn_rb2, L0_ffn_sg, L0_ffn_sgb, L0_ffn_sw1, L0_ffn_sb1, L0_ffn_sw2, L0_ffn_sb2)
    x = x + _L0_attn_b_ref(_layernorm(x, axis=-1), L0_attn_b_in_proj_w, L0_attn_b_conv_w, L0_attn_b_conv_b, L0_attn_b_A_log, L0_attn_b_D, L0_attn_b_dt_bias, L0_attn_b_norm_w, L0_attn_b_out_proj_w)
    x = x + _L0_ffn_ref(_layernorm(x, axis=-1), L0_ffn_wa, L0_ffn_rg, L0_ffn_rgb, L0_ffn_rw1, L0_ffn_rb1, L0_ffn_rw2, L0_ffn_rb2, L0_ffn_sg, L0_ffn_sgb, L0_ffn_sw1, L0_ffn_sb1, L0_ffn_sw2, L0_ffn_sb2)
    return x

_drawn_inputs = setup_inputs


def setup_inputs(seed=0):
    import zlib

    import numpy as np

    out = dict(_drawn_inputs(seed))
    spreads = {'L0_attn_a_dt_bias': (0.0, 0.8),
     'L0_attn_b_conv_b': (0.0, 0.8),
     'L0_attn_b_D': (1.0, 0.6),
     'L0_attn_b_norm_w': (1.0, 0.6),
     'L0_ffn_rgb': (0.0, 0.8),
     'L0_ffn_rb1': (0.0, 0.8),
     'L0_ffn_rb2': (0.0, 0.1),
     'L0_ffn_sgb': (0.0, 0.8),
     'L0_ffn_sb1': (0.0, 0.8),
     'L0_ffn_sb2': (0.0, 0.1)}
    factors = {'L0_attn_b_in_proj_w': 6.047,
     'L0_attn_b_conv_w': 8.0,
     'L0_attn_b_A_log': 8.0,
     'L0_attn_b_dt_bias': 8.0,
     'L0_attn_b_out_proj_w': 5.935,
     'L0_ffn_rg': 7.486,
     'L0_ffn_rw1': 7.411,
     'L0_ffn_rw2': 7.02,
     'L0_ffn_sg': 3.707,
     'L0_ffn_sw1': 3.591,
     'L0_ffn_sw2': 3.439}
    for name, (base, spread) in spreads.items():
        noise = np.random.default_rng([zlib.crc32(name.encode()), seed]).standard_normal(out[name].shape)
        drawn = base * np.exp(spread * noise) if base else spread * noise
        out[name] = jnp.asarray(drawn.astype(out[name].dtype))
    for name, factor in factors.items():
        out[name] = (out[name] * factor).astype(out[name].dtype)
    return out
```

```python
from contextlib import ExitStack

import numpy as np

import concourse.bass as bass
from concourse import mybir
from concourse.alu_op_type import AluOpType as ALU

ACT = mybir.ActivationFunctionType
F32 = mybir.dt.float32
AX_X = mybir.AxisListType.X

P = 128
T, D = 1024, 256
NC = T // P
KD = D // P
TAPS = 4
NS = 128
BANK = 512

HA, PA = 32, 64
PAIRS = HA * PA // P
GROUP = 4
HB, PB = 64, 8
WB = HB * PB
XT = WB // P
BGROUP = 8

E, F, SH = 16, 128, 2
EXPERTS = E + SH

ARENA = 30000
DECAY_FLOOR = -105.0
QUANTUM = 1.5 * 2.0 ** 13
MASKED = -30000.0


class Mark:

    def __init__(self, sem, value):
        self.sem, self.value = sem, value


class Lane:

    def __init__(self, engine, sem):
        self.engine, self.sem, self.count, self.reached = engine, sem, 0, {}

    def wait(self, *marks):
        for m in flat(marks):
            if m.value > self.reached.get(m.sem.name, 0):
                self.engine.wait_ge(m.sem, m.value)
                self.reached[m.sem.name] = m.value

    def do(self, build, *after, mark=True):
        self.wait(*after)
        instruction = build(self.engine)
        if mark:
            instruction.then_inc(self.sem, 1)
            self.count += 1
        return self.last()

    def last(self):
        return Mark(self.sem, self.count)

    def then(self, build, *after):
        return self.do(build, self.last(), *after)

    def copy(self, stream, dst, src, *after):
        self.wait(*after)
        self.engine.dma_start(dst, src).then_inc(stream.sem, 16)
        stream.count += 16
        return Mark(stream.sem, stream.count)


def flat(marks):
    out = []
    for m in marks:
        out += flat(m) if isinstance(m, (list, tuple)) else [m]
    return [m for m in out if m is not None]


class Stream:

    def __init__(self, sem):
        self.sem, self.count = sem, 0


class Ring:

    def __init__(self, buffers):
        self.buffers, self.users, self.n = buffers, [[] for _ in buffers], 0

    def take(self):
        i = self.n % len(self.buffers)
        self.n += 1
        before, self.users[i] = self.users[i], []
        return self.buffers[i], before, self.users[i]


def spread(ap, n):
    return ap.unsqueeze(len(ap.shape)).to_broadcast([*ap.shape, n])


def hybrid_block(nc, io):
    with ExitStack() as ctx:
        def sb(name, shape):
            return ctx.enter_context(nc.sbuf_tensor(name, shape, F32))

        def sem(name):
            return ctx.enter_context(nc.semaphore(name))

        PE, AC, DV, PO, SP = (Lane(engine, sem(f"{name}_done")) for name, engine in (
            ("pe", nc.tensor), ("act", nc.scalar), ("dve", nc.vector), ("pool", nc.gpsimd), ("sp", nc.sync)))

        x = sb("x", [P, NC, D])
        v = sb("v", [P, NC, D])
        vT = sb("vT", [P, KD, T])
        ident = sb("ident", [P, P])
        tri = sb("tri", [P, P])
        ones = sb("ones", [P, P])
        revidx = sb("revidx", [P, E])
        neghalf = sb("neghalf", [P, 2 * NC])
        bn6 = sb("bn6", [P, NC, 6])
        bn2 = sb("bn2", [P, NC, 2])
        rstd = sb("rstd", [P, NC])
        eps_rstd = sb("eps_rstd", [P, NC])
        bcast = [sb(f"bcast{i}", [P, T]) for i in range(4)]
        small = sb("small", [P, 13, 512])
        arena = sb("arena", [P, ARENA])
        psum = ctx.enter_context(nc.psum_tensor("psum", [P, 8 * BANK], F32))
        wide = Ring([psum[:, 2 * i * BANK:(2 * i + 2) * BANK] for i in range(2)])
        work = Ring([psum[:, i * BANK:(i + 1) * BANK] for i in range(4, 8)])

        scratch_a = nc.dram_tensor("scratch_a", [HA, T], F32).ap()
        scratch_b = nc.dram_tensor("scratch_b", [HB, T], F32).ap()
        scratch_e = [nc.dram_tensor(f"scratch_e{i}", [E, T], F32).ap() for i in range(2)]

        streams = {}

        def stream(name):
            if name not in streams:
                streams[name] = Stream(sem(f"dma_{name}"))
            return streams[name]

        bcast_ring = Ring(list(range(len(bcast))))

        def load_rows(row, *after):
            i, before, users = bcast_ring.take()
            m = SP.copy(stream(f"bcast{i}"), bcast[i][:, :], row.to_broadcast([P, T]), before, *after)
            return bcast[i], m, users

        def join():
            marks = [L.last() for L in (PE, AC, DV, PO)] + [Mark(s.sem, s.count) for s in streams.values()]
            for L in (PE, AC, DV, PO, SP):
                L.wait(marks)

        m_x = [SP.copy(stream(f"x{c}"), x[:, c, :], io["x"][c * P:(c + 1) * P, :]) for c in range(NC)]
        m_ident = SP.copy(stream("ident"), ident[:, :], io["ident"])
        m_tri = SP.copy(stream("tri"), tri[:, :], io["tri"])
        m_rev = SP.copy(stream("rev"), revidx[:, :], io["revidx"].to_broadcast([P, E]))
        m_ones = PO.do(lambda e: e.memset(ones[:, :], 1.0))
        m_half = PO.do(lambda e: e.memset(neghalf[:, :], -0.5))

        def layer_norm(m_in, before):
            done = []
            for c in range(NC):
                m = DV.do(lambda e, c=c: e.bn_stats(bn6[:, c, :], x[:, c, :]), m_in[c], before)
                m = DV.do(lambda e, c=c: e.bn_aggr(bn2[:, c, :], bn6[:, c, :]), m)
                m = PO.do(lambda e, c=c: e.tensor_scalar(eps_rstd[:, c:c + 1], bn2[:, c, 1:2], 1e-5, None, ALU.add), m)
                m = PO.do(lambda e, c=c: e.tensor_tensor(rstd[:, c:c + 1], eps_rstd[:, c:c + 1],
                                                         neghalf[:, 0:1], ALU.pow), m, m_half)
                m_v = DV.do(lambda e, c=c: e.tensor_scalar(v[:, c, :], x[:, c, :], bn2[:, c, 0:1], rstd[:, c:c + 1],
                                                           ALU.subtract, ALU.mult), m)
                if c % 2 == 0:
                    bank, free, users = work.take()
                for k in range(KD):
                    o = bank[:, ((c % 2) * KD + k) * P:((c % 2) * KD + k + 1) * P]
                    m = PE.do(lambda e, c=c, k=k, o=o: e.transpose(o, v[:, c, k * P:(k + 1) * P], ident[:, :]),
                              m_v, m_ident, free)
                if c % 2 == 1:
                    m = AC.do(lambda e, c=c, bank=bank: e.copy(
                        vT[:, :, (c - 1) * P:(c + 1) * P].rearrange("p k (c t) -> p c k t", c=2),
                        bank.rearrange("p (c k t) -> p c k t", c=2, k=KD)), m, before)
                    users.append(m)
                    done += [m]
            return [m_v], done

        def softplus(raw, n, dst, tmp, m):
            pos, e_, u, l = (tmp[i][:, 0:n] for i in range(4))
            DV.then(lambda e: e.tensor_scalar(pos, raw, 0.0, None, ALU.max), m)
            m = DV.then(lambda e: e.scalar_tensor_tensor(out=e_, in0=pos, scalar=-2.0, in1=raw, op0=ALU.mult, op1=ALU.add))
            m = AC.do(lambda e: e.activation(e_, e_, ACT.Exp), m)
            m = DV.do(lambda e: e.tensor_scalar(u, e_, 1.0, None, ALU.add), m)
            m_l = AC.do(lambda e: e.activation(l, u, ACT.Ln), m)
            DV.then(lambda e: e.scalar_tensor_tensor(out=e_, in0=u, scalar=-1.0, in1=e_, op0=ALU.add, op1=ALU.subtract))
            DV.then(lambda e: e.tensor_tensor(pos, pos, l, ALU.add), m_l)
            DV.then(lambda e: e.reciprocal(u, u), m_l)
            DV.then(lambda e: e.tensor_tensor(u, u, e_, ALU.mult))
            return DV.then(lambda e: e.tensor_tensor(dst, pos, u, ALU.subtract))

        def decays(H, raw, m_raw, a_log, m_alog, scratch):
            n = H * NC
            f = {}
            for i, name in enumerate(("dt", "t0", "t1", "t2", "t3", "hi", "lo", "cumhi", "cumlo", "tothi",
                                      "totlo", "wd", "dec")):
                f[name] = small[:, i, 0:n]
            m = softplus(raw, n, f["dt"], [small[:, i, :] for i in range(1, 5)], m_raw)
            a = f["t0"]
            m_ea = AC.do(lambda e: e.activation(a_log, a_log, ACT.Exp), m_alog)
            DV.then(lambda e: e.scalar_tensor_tensor(out=a.rearrange("p (h c) -> p h c", c=NC),
                                                     in0=f["dt"].rearrange("p (h c) -> p h c", c=NC), scalar=-1.0,
                                                     in1=spread(a_log, NC), op0=ALU.mult, op1=ALU.mult), m_ea)
            DV.then(lambda e: e.tensor_scalar(a, a, DECAY_FLOOR, None, ALU.max))
            DV.then(lambda e: e.tensor_scalar(f["hi"], a, QUANTUM, None, ALU.add))
            DV.then(lambda e: e.tensor_scalar(f["hi"], f["hi"], QUANTUM, None, ALU.subtract))
            m = DV.then(lambda e: e.tensor_tensor(f["lo"], a, f["hi"], ALU.subtract))
            for lhs, m_lhs, src, dst in ((tri, m_tri, "hi", "cumhi"), (tri, m_tri, "lo", "cumlo"),
                                         (ones, m_ones, "hi", "tothi"), (ones, m_ones, "lo", "totlo")):
                bank, free, users = work.take()
                mp = PE.do(lambda e, lhs=lhs, src=src, bank=bank: e.matmul(bank[:, 0:n], lhs[:, :], f[src],
                                                                           start=True, stop=True), m, m_lhs, free)
                m_c = DV.do(lambda e, dst=dst, bank=bank: e.tensor_copy(f[dst], bank[:, 0:n]), mp)
                users.append(m_c)
                if dst == "cumhi":
                    bank, free, users = work.take()
                    for q in range(n // P):
                        mp = PE.do(lambda e, q=q, bank=bank: e.transpose(
                            bank[:, q * P:(q + 1) * P], f["cumhi"][:, q * P:(q + 1) * P], ident[:, :]), m_c, m_ident, free)
                    rows = f["t1"]
                    m_r = DV.do(lambda e, bank=bank: e.tensor_copy(rows, bank[:, 0:n]), mp)
                    users.append(m_r)
                    m_scr = SP.copy(stream("scratch"), scratch.rearrange("(q g) (c t) -> (g c) q t", q=n // P, c=NC),
                                    rows.rearrange("p (q t) -> p q t", t=P), m_r)
            AC.do(lambda e: e.activation(f["t2"], f["cumlo"], ACT.Exp), DV.last())
            m = AC.do(lambda e: e.activation(f["t3"], f["cumlo"], ACT.Exp, scale=-1.0))
            f["elo"], f["ehi"] = f["t2"], f["t0"]
            m_dtl = DV.then(lambda e: e.tensor_tensor(f["t3"], f["t3"], f["dt"], ALU.mult), m)
            f["dtl"] = f["t3"]
            AC.do(lambda e: e.activation(f["ehi"], f["cumhi"], ACT.Exp))
            DV.then(lambda e: e.tensor_tensor(f["wd"], f["tothi"], f["cumhi"], ALU.subtract))
            DV.then(lambda e: e.tensor_tensor(f["wd"], f["wd"], f["totlo"], ALU.add))
            m = DV.then(lambda e: e.tensor_tensor(f["dec"], f["tothi"], f["totlo"], ALU.add))
            AC.do(lambda e: e.activation(f["wd"], f["wd"], ACT.Exp), m)
            m = AC.do(lambda e: e.activation(f["dec"], f["dec"], ACT.Exp))
            return f, [m, m_dtl], m_scr

        def conv(tile_out, bank, m_pe, w, m_w, free, users, bias=None):
            m = AC.do(lambda e: e.activation(tile_out, bank, ACT.Identity, scale=w[:, TAPS - 1:TAPS],
                                             bias=0.0 if bias is None else bias), m_pe, m_w, free)
            for s in range(1, TAPS):
                m = DV.then(lambda e, s=s: e.scalar_tensor_tensor(
                    out=tile_out[:, s:T], in0=bank[:, 0:T - s], scalar=w[:, TAPS - 1 - s:TAPS - s],
                    in1=tile_out[:, s:T], op0=ALU.mult, op1=ALU.add), m, m_w)
            users.append(m)
            return AC.do(lambda e: e.activation(tile_out, tile_out, ACT.Silu), m)

        def project(weight, m_w, m_vT):
            bank, free, users = wide.take()
            for half in range(2):
                for k in range(KD):
                    m = PE.do(lambda e, k=k, half=half: e.matmul(
                        bank[:, half * BANK:(half + 1) * BANK], weight(k), vT[:, k, half * BANK:(half + 1) * BANK],
                        start=(k == 0), stop=(k == KD - 1)), m_w, m_vT, free, mark=(half == 1 and k == KD - 1))
            return bank, m, users

        def decay_matrix(rows, m_rows, cum, m_cum, on_vector):
            r3 = rows[:, :].rearrange("p (c t) -> p c t", t=P)
            lane = DV if on_vector else PO
            m = lane.do(lambda e: e.tensor_tensor(r3, r3, spread(cum, P), ALU.subtract), m_rows, m_cum)
            m = PO.do(lambda e: e.affine_select(out=r3, in_=r3, compare_op=ALU.is_ge, fill=MASKED, base=0,
                                                pattern=[[0, NC], [1, P]], channel_multiplier=-1), m)
            return AC.do(lambda e: e.activation(rows[:, :], rows[:, :], ACT.Exp), m)

        class Arena:
            def __init__(self):
                self.at = 0

            def __call__(self, n):
                self.at += n
                assert self.at <= ARENA, self.at
                return arena[:, self.at - n:self.at]

        A = Arena()
        TILES = 6
        w_ring = Ring([A(KD * TILES * P).rearrange("p (k i m) -> p k i m", k=KD, i=TILES) for _ in range(2)])
        cv_ring = Ring([A(TILES * T).rearrange("p (i t) -> p i t", i=TILES) for _ in range(2)])
        cw = A(PAIRS * 5 * TAPS).rearrange("p (j i k) -> p j i k", i=5, k=TAPS)
        wdt = A(KD * HA).rearrange("p (k h) -> p k h", k=KD)
        dtb, alog = A(HA), A(HA)
        raw_a = A(HA * NC)
        u_ring = Ring([(A(T).rearrange("p (c m) -> p c m", c=NC), A(T).rearrange("p (c m) -> p c m", c=NC))])
        bt_ring = Ring([A(T) for _ in range(2)])
        st_ring = Ring([A(NC * PA).rearrange("p (c m) -> p c m", c=NC) for _ in range(2)])
        y_ring = Ring([A(T).rearrange("p (c m) -> p c m", c=NC)])
        y2 = A(T)
        elo2 = A(HA * NC)
        gated = Ring([A(GROUP * T).rearrange("p (g t) -> p g t", g=GROUP)])
        wout_ring = Ring([A(GROUP * D).rearrange("p (g d) -> p g d", g=GROUP)])
        nrm = [A(2 * NC) for _ in range(2)]

        m_cw = SP.copy(stream("cw"), cw, io["conv_a"])
        m_wdt = SP.copy(stream("wdt"), wdt, io["wdt_a"])
        m_dtb = SP.copy(stream("dtb"), dtb, io["dtb_a"].to_broadcast([P, HA]))
        m_alog = SP.copy(stream("alog"), alog, io["alog_a"].to_broadcast([P, HA]))
        wq = {}

        def load_pair(j):
            w, before, users = w_ring.take()
            wq[j] = (w, SP.copy(stream(f"wa{j % 2}"), w, io["w_a"][j], before), users)

        load_pair(0)
        load_pair(1)
        m_zero = [PO.do(lambda e, b=b: e.memset(b[:, 0, :], 0.0)) for b in st_ring.buffers]

        _, m_vT = layer_norm(m_x, None)

        def project_dt(wdt, m_wdt, H, bias, m_bias, raw):
            bank, free, users = work.take()
            for c in range(NC):
                for k in range(KD):
                    m = PE.do(lambda e, c=c, k=k: e.matmul(bank[:, c * H:(c + 1) * H], vT[:, k, c * P:(c + 1) * P],
                                                           wdt[:, k, :], start=(k == 0), stop=(k == KD - 1)),
                              m_vT[c // 2], m_wdt, free, mark=(c == NC - 1))
            m = DV.do(lambda e: e.tensor_tensor(raw.rearrange("p (h c) -> p h c", c=NC),
                                                bank[:, 0:H * NC].rearrange("p (c h) -> p h c", c=NC),
                                                spread(bias, NC), ALU.add), m, m_bias)
            users.append(m)
            return m

        m = project_dt(wdt, m_wdt, HA, dtb, m_dtb, raw_a)
        fa, m_fa, m_scr = decays(HA, raw_a, m, alog, m_alog, scratch_a)
        m = DV.then(lambda e: e.tensor_tensor(elo2, fa["elo"], fa["elo"], ALU.mult), m_fa)
        m_fa = [m_fa, DV.then(lambda e: e.tensor_scalar(elo2, elo2, 1.0 / PA, None, ALU.mult))]

        def fac(name, h):
            return fa[name][:, h * NC:(h + 1) * NC]

        conv_out = {}

        def project_tiles(j):
            w, m_w, w_users = wq.pop(j)
            out, free, users = cv_ring.take()
            marks = []
            conv_out[j] = (out, marks, users)
            for i in range(TILES):
                bank, m, b_users = project(lambda k, i=i: w[:, k, i, :], m_w, m_vT)
                if i == TILES - 1:
                    w_users.append(m)
                    m = AC.do(lambda e, i=i, bank=bank: e.activation(out[:, i, :], bank, ACT.Silu), m, free)
                    b_users.append(m)
                    marks.append(m)
                else:
                    marks.append(conv(out[:, i, :], bank, m, cw[:, j, i, :], m_cw, free, b_users))
                yield
            if j + 2 < PAIRS:
                load_pair(j + 2)

        rows = {}

        def decay_pair(j):
            for g in range(2):
                h = 2 * j + g
                buf, m, users = load_rows(scratch_a[h:h + 1, :], m_scr)
                rows[h] = (buf, decay_matrix(buf, m, fac("cumhi", h), m_fa, False), users)

        group = {}

        def scan_pair(j):
            out, m_cv, cv_users = conv_out.pop(j)
            (U, Ud), u_free, u_users = u_ring.take()
            m_u = []
            for q in range(2):
                bank, free, users = work.take()
                cs = slice(4 * q, 4 * q + 4)
                for c in range(4 * q, 4 * q + 4):
                    m = PE.do(lambda e, c=c: e.transpose(bank[:, (c % 4) * P:(c % 4 + 1) * P],
                                                         out[:, 0, c * P:(c + 1) * P], ident[:, :]),
                              m_cv[0], free, mark=(c % 4 == 3))
                for dst, name, src, lane in ((U, "dtl", bank.rearrange("p (c m) -> p c m", c=4), DV),
                                             (Ud, "wd", U[:, cs, :], PO)):
                    for g in range(2):
                        sl = slice(g * PA, (g + 1) * PA)
                        m = lane.do(lambda e, dst=dst, name=name, src=src, g=g, sl=sl, cs=cs: e.tensor_tensor(
                            dst[:, cs, sl], src[:, :, sl], spread(fac(name, 2 * j + g)[:, cs], PA), ALU.mult),
                            m, m_fa, u_free)
                    if lane is DV:
                        users.append(m)
                m_u.append(m)
                yield
            y, y_free, y_users = y_ring.take()
            m_y = []
            for g in range(2):
                h = 2 * j + g
                bt, bt_free, bt_users = bt_ring.take()
                m_bt = []
                for q in range(2):
                    bank, free, users = work.take()
                    for c in range(4 * q, 4 * q + 4):
                        m = PE.do(lambda e, c=c: e.transpose(bank[:, (c % 4) * P:(c % 4 + 1) * P],
                                                             out[:, 1 + g, c * P:(c + 1) * P], ident[:, :]),
                                  m_cv[1 + g], free, mark=(c % 4 == 3))
                    m = AC.do(lambda e, q=q, bank=bank: e.copy(bt[:, q * BANK:(q + 1) * BANK], bank), m, bt_free)
                    users.append(m)
                    m_bt.append(m)
                yield
                buf, m_e, e_users = rows.pop(h)
                m_m = []
                for q in range(2):
                    bank, free, users = work.take()
                    for c in range(4 * q, 4 * q + 4):
                        m = PE.do(lambda e, c=c: e.matmul(bank[:, (c % 4) * P:(c % 4 + 1) * P],
                                                          out[:, 1 + g, c * P:(c + 1) * P],
                                                          out[:, 3 + g, c * P:(c + 1) * P], start=True, stop=True),
                                  m_cv[1 + g], m_cv[3 + g], free, mark=(c % 4 == 3))
                    m = DV.do(lambda e, q=q, bank=bank: e.tensor_tensor(
                        buf[:, q * BANK:(q + 1) * BANK], bank, buf[:, q * BANK:(q + 1) * BANK], ALU.mult), m, m_e)
                    users.append(m)
                    m_m.append(m)
                yield
                hs = slice(g * PA, (g + 1) * PA)
                bank_s, free, users_s = work.take()
                for c in range(NC - 1):
                    m = PE.do(lambda e, c=c: e.matmul(bank_s[:, c * PA:(c + 1) * PA], bt[:, c * P:(c + 1) * P],
                                                      Ud[:, c, hs], start=True, stop=True),
                              m_bt, m_u, free, mark=(c == NC - 2))
                bt_users.append(m)
                m_s = m
                st, st_free, st_users = st_ring.take()
                for c in range(NC - 1):
                    m = DV.then(lambda e, c=c: e.scalar_tensor_tensor(
                        out=st[:, c + 1, :], in0=st[:, c, :], scalar=fac("dec", h)[:, c:c + 1],
                        in1=bank_s[:, c * PA:(c + 1) * PA], op0=ALU.mult, op1=ALU.add), m_s, m_fa, st_free, m_zero)
                users_s.append(m)
                m_st = m
                bank_i, free, users_i = work.take()
                for c in range(NC):
                    m = PE.do(lambda e, c=c: e.matmul(bank_i[:, c * PA:(c + 1) * PA], buf[:, c * P:(c + 1) * P],
                                                      U[:, c, hs], start=True, stop=True),
                              m_m, m_u, free, mark=(c == NC - 1))
                e_users.append(m)
                m_i = m
                yield
                bank_x, free, users_x = work.take()
                for c in range(NC):
                    m = PE.do(lambda e, c=c: e.matmul(bank_x[:, c * PA:(c + 1) * PA], out[:, 3 + g, c * P:(c + 1) * P],
                                                      st[:, c, :], start=True, stop=True),
                              m_st, free, mark=(c == NC - 1))
                st_users.append(m)
                m = DV.do(lambda e: e.tensor_tensor(y[:, :, hs], bank_x.rearrange("p (c m) -> p c m", c=NC),
                                                    spread(fac("ehi", h), PA), ALU.mult), m, y_free)
                users_x.append(m)
                m = DV.do(lambda e: e.tensor_tensor(y[:, :, hs], bank_i.rearrange("p (c m) -> p c m", c=NC),
                                                    y[:, :, hs], ALU.add), m, m_i)
                users_i.append(m)
                m_y.append(m)
                yield
            u_users.append(PE.last())
            y2v = y2.rearrange("p (c m) -> p c m", c=NC)
            m = PO.do(lambda e: e.tensor_tensor(y2v, y, y, ALU.mult), m_y, DV.last())
            m = DV.do(lambda e: e.tensor_reduce(nrm[0].rearrange("p (g c) -> p g c", g=2),
                                                y2.rearrange("p (c g m) -> p g c m", c=NC, g=2), AX_X, ALU.add), m)
            pr = slice(2 * j * NC, (2 * j + 2) * NC)
            m = PO.do(lambda e: e.tensor_tensor(nrm[1], nrm[0], elo2[:, pr], ALU.mult), m)
            m = PO.do(lambda e: e.tensor_scalar(nrm[1], nrm[1], 1e-6, None, ALU.add), m)
            m = PO.do(lambda e: e.tensor_tensor(nrm[1], nrm[1], neghalf[:, 0:2 * NC], ALU.pow), m)
            m = PO.do(lambda e: e.tensor_tensor(nrm[1], nrm[1], fa["elo"][:, pr], ALU.mult), m)
            for g in range(2):
                hs = slice(g * PA, (g + 1) * PA)
                m = PO.do(lambda e, g=g, hs=hs: e.tensor_tensor(y[:, :, hs], y[:, :, hs],
                                                                spread(nrm[1][:, g * NC:(g + 1) * NC], PA), ALU.mult), m)
            yield
            if j % GROUP == 0:
                gt, g_free, g_users = gated.take()
                wo, w_free, w_users = wout_ring.take()
                m_wo = SP.copy(stream("wo"), wo, io["wout_a"][j // GROUP], w_free)
                group.update(gt=gt, free=g_free, users=g_users, wo=wo, m_wo=m_wo, w_users=w_users)
            gt, wo = group["gt"], group["wo"]
            for q in range(2):
                bank, free, users = work.take()
                for c in range(4 * q, 4 * q + 4):
                    mp = PE.do(lambda e, c=c: e.transpose(bank[:, (c % 4) * P:(c % 4 + 1) * P], y[:, c, :], ident[:, :]),
                               m, free, mark=(c % 4 == 3))
                mg = DV.do(lambda e, q=q, bank=bank: e.tensor_tensor(
                    gt[:, j % GROUP, q * BANK:(q + 1) * BANK], bank, out[:, 5, q * BANK:(q + 1) * BANK], ALU.mult),
                    mp, m_cv[5], group["free"])
                users.append(mg)
            y_users.append(mp)
            cv_users += [mg, PE.last()]
            yield
            if j % GROUP == GROUP - 1:
                for q in range(NC // 2):
                    bank, free, users = work.take()
                    for c in (2 * q, 2 * q + 1):
                        for g in range(GROUP):
                            mp = PE.do(lambda e, c=c, g=g, bank=bank: e.matmul(
                                bank[:, (c % 2) * D:(c % 2 + 1) * D], gt[:, g, c * P:(c + 1) * P], wo[:, g, :],
                                start=(g == 0), stop=(g == GROUP - 1)), mg, group["m_wo"], free,
                                mark=(c % 2 == 1 and g == GROUP - 1))
                    mx = DV.do(lambda e, q=q, bank=bank: e.tensor_tensor(
                        x[:, 2 * q:2 * q + 2, :], bank.rearrange("p (c d) -> p c d", c=2), x[:, 2 * q:2 * q + 2, :],
                        ALU.add), mp, m_xa[q])
                    m_xa[q] = mx
                    users.append(mx)
                group["users"].append(mp)
                group["w_users"].append(mp)
                yield

        m_xa = [None] * (NC // 2)

        def interleave(*steps):
            live = [s for s in steps if s is not None]
            while live:
                for s in list(live):
                    if next(s, live) is live:
                        live.remove(s)

        interleave(project_tiles(0))
        for j in range(PAIRS):
            decay_pair(j)
            interleave(scan_pair(j), project_tiles(j + 1) if j + 1 < PAIRS else None)
        m_xa = [m_xa[c // 2] for c in range(NC)]
        join()

        def experts(n, m_in):
            G = Arena()
            wg_ring = Ring([tuple(G(KD * F).rearrange("p (k f) -> p k f", k=KD) for _ in range(2)) + (G(D),)
                            for _ in range(4)])
            wa = G(KD * E).rearrange("p (k e) -> p k e", k=KD)
            gb, ub = G(EXPERTS), G(EXPERTS)
            aff, key, one, comb, c2 = (G(NC * E).rearrange("p (e c) -> p e c", c=NC) for _ in range(5))
            m1, m2, km, den = (G(NC) for _ in range(4))
            combT = G(T)
            b2w = G(D)
            gate_ring = Ring([G(BANK) for _ in range(3)])
            hid_ring = Ring([G(BANK) for _ in range(3)])
            wq = {}
            order = list(range(E, EXPERTS)) + list(range(E))

            def load_expert(p):
                i = order[p]
                w, before, users = wg_ring.take()
                got = []
                for part, name in zip(w, ("wg", "wu", "wd")):
                    m = SP.copy(stream(f"{name}{p % 4}"), part, io[name][i], before)
                    got.append(m)
                wq[i] = (w, got, users)

            m_wa = SP.copy(stream("wa_e"), wa, io["wa_e"])
            m_gb = SP.copy(stream("gb"), gb, io["gb"])
            m_ub = SP.copy(stream("ub"), ub, io["ub"])
            m_b2 = SP.copy(stream("b2"), b2w[0:EXPERTS, :], io["b2"])
            for i in range(3):
                load_expert(i)
            m_v, m_vT = layer_norm(m_in, None)

            bank, free, users = work.take()
            for c in range(NC):
                for k in range(KD):
                    m = PE.do(lambda e, c=c, k=k: e.matmul(bank[:, c * E:(c + 1) * E], vT[:, k, c * P:(c + 1) * P],
                                                           wa[:, k, :], start=(k == 0), stop=(k == KD - 1)),
                              m_vT[c // 2], m_wa, free, mark=(c == NC - 1))
            m = AC.do(lambda e: e.activation(aff, bank[:, 0:NC * E].rearrange("p (c e) -> p e c", c=NC), ACT.Exp,
                                             scale=-1.0), m)
            users.append(m)
            DV.do(lambda e: e.tensor_scalar(aff, aff, 1.0, None, ALU.add), m)
            DV.then(lambda e: e.reciprocal(aff, aff))

            def by_chunk(ap):
                return ap.rearrange("p e c -> p c e")

            def over_e(ap):
                return ap.unsqueeze(1).to_broadcast([P, E, NC])

            def first_best(src, best, onehot):
                DV.then(lambda e: e.tensor_reduce(best, by_chunk(src), AX_X, ALU.max))
                DV.then(lambda e: e.tensor_tensor(key, src, over_e(best), ALU.is_equal))
                DV.then(lambda e: e.tensor_tensor(by_chunk(key), by_chunk(key),
                                                  revidx[:, :].unsqueeze(1).to_broadcast([P, NC, E]), ALU.mult), m_rev)
                DV.then(lambda e: e.tensor_reduce(km, by_chunk(key), AX_X, ALU.max))
                DV.then(lambda e: e.tensor_tensor(onehot, key, over_e(km), ALU.is_equal))

            first_best(aff, m1, one)
            DV.then(lambda e: e.tensor_tensor(comb, one, over_e(m1), ALU.mult))
            DV.then(lambda e: e.scalar_tensor_tensor(out=aff, in0=one, scalar=-4.0, in1=aff, op0=ALU.mult, op1=ALU.add))
            first_best(aff, m2, one)
            DV.then(lambda e: e.tensor_tensor(c2, one, over_e(m2), ALU.mult))
            DV.then(lambda e: e.tensor_tensor(comb, comb, c2, ALU.add))
            DV.then(lambda e: e.tensor_tensor(den, m1, m2, ALU.add))
            DV.then(lambda e: e.reciprocal(den, den))
            m = DV.then(lambda e: e.tensor_tensor(comb, comb, over_e(den), ALU.mult))
            bank, free, users = work.take()
            m = PE.do(lambda e: e.transpose(bank[:, 0:P], comb.rearrange("p e c -> p (e c)"), ident[:, :]), m, free)
            m = DV.do(lambda e: e.tensor_copy(c2.rearrange("p e c -> p (e c)"), bank[:, 0:P]), m)
            users.append(m)
            m_scr = SP.copy(stream("scratch"), scratch_e[n].rearrange("e (c t) -> (e c) t", c=NC),
                            c2.rearrange("p e c -> p (e c)"), m)
            m = DV.do(lambda e: e.memset(combT[0:EXPERTS, :], 1.0))
            m_cT = SP.copy(stream("combT"), combT[0:E, :], scratch_e[n], m, m_scr)
            m_res = PO.do(lambda e: e.tensor_tensor(x[:, :, :], x[:, :, :], v[:, :, :], ALU.add), m_v)

            banks = [psum[:, i * BANK:(i + 1) * BANK] for i in range(8)]
            out_free = flat([work.users[i] for i in range(4)])
            up = Ring([(psum[:, 0:BANK], psum[:, BANK:2 * BANK]), (psum[:, 2 * BANK:3 * BANK], psum[:, 3 * BANK:4 * BANK])])
            up.users = [list(wide.users[0]), list(wide.users[1])]
            hidden, rowsof = {}, {}

            def up_half(i, half):
                (wg, wu, wd), m_w, _ = wq[i]
                (bg, bu), free, users = up.take()
                for bank, w in ((bg, wg), (bu, wu)):
                    for k in range(KD):
                        m = PE.do(lambda e, k=k, bank=bank, w=w: e.matmul(
                            bank, w[:, k, :], vT[:, k, half * BANK:(half + 1) * BANK], start=(k == 0), stop=(k == KD - 1)),
                            m_w, m_vT, free, mark=(k == KD - 1))
                gate, g_free, g_users = gate_ring.take()
                hid, h_free, h_users = hid_ring.take()
                m_g = AC.do(lambda e: e.activation(gate, bg, ACT.Gelu, bias=gb[:, i:i + 1]), m, m_gb, g_free)
                if i < E:
                    rb, m_rb, rb_users = rowsof[i]
                    m_g = PO.do(lambda e: e.tensor_tensor(gate, gate, rb[:, half * BANK:(half + 1) * BANK], ALU.mult),
                                m_g, m_rb)
                    rb_users.append(m_g)
                m = DV.do(lambda e: e.scalar_tensor_tensor(out=hid, in0=bu, scalar=ub[:, i:i + 1], in1=gate,
                                                           op0=ALU.add, op1=ALU.mult), m, m_g, m_ub, h_free)
                users += [m, m_g]
                g_users.append(m)
                hidden[i, half] = (hid, m, h_users)

            def out_cols(c):
                return psum[:, 4 * BANK + c * D:4 * BANK + (c + 1) * D]

            def down_half(i, half):
                (wg, wu, wd), m_w, w_users = wq[i]
                hid, m_h, h_users = hidden.pop((i, half))
                for c in range(4 * half, 4 * half + 4):
                    m = PE.do(lambda e, c=c: e.matmul(out_cols(c), hid[:, (c % 4) * P:(c % 4 + 1) * P], wd,
                                                      start=False, stop=(i == order[-1]), skip_group_check=True),
                              m_h, mark=(c % 4 == 3))
                h_users.append(m)
                if half == 1:
                    w_users.append(m)
                return m

            steps = [(i, half) for i in order for half in range(2)]
            for s, (i, half) in enumerate(steps):
                if half == 0:
                    p = order.index(i)
                    for nxt in order[p:p + 3]:
                        if nxt < E and nxt not in rowsof:
                            rowsof[nxt] = load_rows(scratch_e[n][nxt:nxt + 1, :], m_scr)
                up_half(i, half)
                if s == 2:
                    for c in range(NC):
                        PE.do(lambda e, c=c: e.matmul(out_cols(c), combT[0:EXPERTS, c * P:(c + 1) * P],
                                                      b2w[0:EXPERTS, :], start=(c % 2 == 0), stop=False,
                                                      skip_group_check=True), m_cT, m_b2, out_free)
                if s >= 2:
                    down_half(*steps[s - 2])
                if half == 1 and s // 2 + 3 < len(order):
                    load_expert(s // 2 + 3)
            m_last = [down_half(*s) for s in steps[-2:]]
            m_out = []
            for q in range(4):
                m = DV.do(lambda e, q=q: e.tensor_tensor(
                    x[:, 2 * q:2 * q + 2, :], banks[4 + q].rearrange("p (c d) -> p c d", c=2),
                    x[:, 2 * q:2 * q + 2, :], ALU.add), m_last[q // 2], m_res)
                m_out += [m, m]
            join()
            return m_out


        m_x1 = experts(0, m_xa)

        B = Arena()
        w_ring = Ring([B(KD * P).rearrange("p (k m) -> p k m", k=KD) for _ in range(3)])
        cw = B(6 * TAPS).rearrange("p (i k) -> p i k", k=TAPS)
        cb, nw = B(6), B(XT)
        wdt = B(KD * HB).rearrange("p (k h) -> p k h", k=KD)
        dtb, alog, dskip = B(HB), B(HB), B(HB)
        xt = B(XT * T).rearrange("p (i t) -> p i t", i=XT)
        zc = B(XT * T).rearrange("p (i t) -> p i t", i=XT)
        Bt, Ct, Bs, G = B(T), B(T), B(T), B(T)
        U = B(NC * WB).rearrange("p (c m) -> p c m", c=NC)
        Dx = B(NC * WB).rearrange("p (c m) -> p c m", c=NC)
        y = B(NC * WB).rearrange("p (c m) -> p c m", c=NC)
        ud_ring = Ring([B(WB) for _ in range(2)])
        st_ring = Ring([B(WB) for _ in range(2)])
        wout = B(XT * D).rearrange("p (i d) -> p i d", i=XT)
        ssq, rms = B(NC), B(NC)
        raw_b = y.rearrange("p c m -> p (c m)")[:, 0:HB * NC]

        m_cw = SP.copy(stream("cw"), cw, io["conv_b"])
        m_cb = SP.copy(stream("cb"), cb, io["convbias_b"])
        m_nw = SP.copy(stream("nw"), nw, io["norm_b"])
        m_wdt = SP.copy(stream("wdt"), wdt, io["wdt_b"])
        m_dtb = SP.copy(stream("dtb"), dtb, io["dtb_b"].to_broadcast([P, HB]))
        m_alog = SP.copy(stream("alog"), alog, io["alog_b"].to_broadcast([P, HB]))
        m_dsk = SP.copy(stream("dskip"), dskip, io["d_b"].to_broadcast([P, HB]))
        m_wout = SP.copy(stream("wo"), wout, io["wout_b"])
        m_cw = DV.do(lambda e: e.tensor_scalar(cw, cw, 0.5, None, ALU.mult), m_cw)
        _, m_vT = layer_norm(m_x1, None)

        def project_b(i):
            w, before, users = w_ring.take()
            m_w = SP.copy(stream(f"wb{i % 3}"), w, io["w_b"][i], before)
            bank, m, b_users = project(lambda k: w[:, k, :], m_w, m_vT)
            users.append(m)
            return bank, m, b_users

        m = project_dt(wdt, m_wdt, HB, dtb, m_dtb, raw_b)
        fb, m_fb, m_scr = decays(HB, raw_b, m, alog, m_alog, scratch_b)
        m_cv = []
        for i, dst in enumerate([Bt, Ct] + [xt[:, q, :] for q in range(XT)]):
            bank, m, users = project_b(i)
            m_cv.append(conv(dst, bank, m, cw[:, i, :], [m_cw, m_cb], None, users, bias=cb[:, i:i + 1]))
        m_z = []
        for q in range(XT):
            bank, m, users = project_b(6 + q)
            m = AC.do(lambda e, q=q, bank=bank: e.activation(zc[:, q, :], bank, ACT.Silu, scale=0.25), m)
            users.append(m)
            m_z.append(m)

        m_bs, m_g, m_u = [], [], []
        for q in range(2):
            bank, free, users = work.take()
            for c in range(4 * q, 4 * q + 4):
                m = PE.do(lambda e, c=c, bank=bank: e.transpose(bank[:, (c % 4) * P:(c % 4 + 1) * P],
                                                                Bt[:, c * P:(c + 1) * P], ident[:, :]), m_cv[0], free)
            m = AC.do(lambda e, q=q, bank=bank: e.copy(Bs[:, q * BANK:(q + 1) * BANK], bank), m)
            users.append(m)
            m_bs.append(m)
            bank, free, users = work.take()
            for c in range(4 * q, 4 * q + 4):
                m = PE.do(lambda e, c=c, bank=bank: e.matmul(bank[:, (c % 4) * P:(c % 4 + 1) * P],
                                                             Bt[:, c * P:(c + 1) * P], Ct[:, c * P:(c + 1) * P],
                                                             start=True, stop=True), m_cv[0:2], free)
            m = AC.do(lambda e, q=q, bank=bank: e.copy(G[:, q * BANK:(q + 1) * BANK], bank), m)
            users.append(m)
            m_g.append(m)

        def per_head(name, c):
            return spread(fb[name].rearrange("p (h c) -> p h c", c=NC)[:, :, c], PB)

        def heads(ap):
            return ap.rearrange("p (h m) -> p h m", m=PB)

        for c in range(NC):
            bank, free, users = work.take()
            for i in range(XT):
                m = PE.do(lambda e, i=i, c=c, bank=bank: e.transpose(bank[:, i * P:(i + 1) * P],
                                                                     xt[:, i, c * P:(c + 1) * P], ident[:, :]),
                          m_cv[2 + i], free)
            m_t = m
            m = DV.do(lambda e, c=c, bank=bank: e.tensor_tensor(heads(U[:, c, :]), heads(bank), per_head("dtl", c),
                                                                ALU.mult), m_t, m_fb)
            m_u.append(m)
            m = DV.do(lambda e, c=c, bank=bank: e.tensor_tensor(heads(Dx[:, c, :]), heads(bank),
                                                                spread(dskip, PB), ALU.mult), m_t, m_dsk)
            users.append(m)

        m_y = []
        m_y.append(PO.do(lambda e: e.memset(y[:, 0, :], 0.0), m_fb))
        st_prev, m_st = None, None
        for c in range(NC - 1):
            (ud, ud_free, ud_users), (st, st_free, st_users) = ud_ring.take(), st_ring.take()
            m = PO.do(lambda e, c=c, ud=ud: e.tensor_tensor(heads(ud), heads(U[:, c, :]), per_head("wd", c), ALU.mult),
                      m_u[c], m_fb, ud_free)
            bank, free, users = work.take()
            m = PE.do(lambda e, c=c, ud=ud, bank=bank: e.matmul(bank, Bs[:, c * P:(c + 1) * P], ud,
                                                                start=True, stop=True), m, m_bs, free)
            ud_users.append(m)
            if c == 0:
                m_st = DV.do(lambda e, st=st, bank=bank: e.tensor_copy(st, bank), m, st_free)
            else:
                md = DV.do(lambda e, c=c, st=st, old=st_prev: e.tensor_tensor(heads(st), heads(old), per_head("dec", c),
                                                                             ALU.mult), m_st, st_free, m_fb)
                m_st = DV.do(lambda e, st=st, bank=bank: e.tensor_tensor(st, bank, st, ALU.add), m, md)
                st_prev_users.append(m_st)
            users.append(m_st)
            st_prev, st_prev_users = st, st_users
            bank, free, users = work.take()
            m = PE.do(lambda e, c=c, st=st, bank=bank: e.matmul(bank, Ct[:, (c + 1) * P:(c + 2) * P], st,
                                                                start=True, stop=True), m_st, m_cv[1], free)
            st_users.append(m)
            m = DV.do(lambda e, c=c, bank=bank: e.tensor_tensor(heads(y[:, c + 1, :]), heads(bank),
                                                                per_head("ehi", c + 1), ALU.mult), m, m_fb)
            users.append(m)
            m_y.append(m)

        rows, ready = {}, {}

        def load_head(h):
            rows[h] = load_rows(scratch_b[h:h + 1, :], m_scr)

        def decay_head(h):
            buf, m, users = rows[h]
            ready[h] = decay_matrix(buf, m, fb["cumhi"][:, h * NC:(h + 1) * NC], m_fb, h % 2 == 1)

        load_head(0)
        load_head(1)
        load_head(2)
        decay_head(0)
        m_yb = []
        for h in range(HB):
            if h % BGROUP == 0:
                bank, free, b_users = work.take()
            if h + 3 < HB:
                load_head(h + 3)
            if h + 1 < HB:
                decay_head(h + 1)
            buf, _, users = rows.pop(h)
            m = DV.do(lambda e, buf=buf: e.tensor_tensor(buf[:, :], buf[:, :], G, ALU.mult), ready.pop(h), m_g)
            o = bank.rearrange("p (c m) -> p c m", c=NC)
            for c in range(NC):
                hs = slice(h * PB, (h + 1) * PB)
                gs = slice((h % BGROUP) * PB, (h % BGROUP + 1) * PB)
                m = PE.do(lambda e, c=c, buf=buf, hs=hs, gs=gs, o=o: e.matmul(
                    o[:, c, gs], buf[:, c * P:(c + 1) * P], U[:, c, hs], start=True, stop=True), m, m_u, free,
                    mark=(c == NC - 1))
            users.append(m)
            if h % BGROUP == BGROUP - 1:
                g = h // BGROUP
                ws = slice(g * BGROUP * PB, (g + 1) * BGROUP * PB)
                m = DV.do(lambda e, o=o, ws=ws: e.tensor_tensor(y[:, :, ws], o, y[:, :, ws], ALU.add), m, m_y)
                b_users.append(m)
                for hh in range(g * BGROUP, (g + 1) * BGROUP):
                    hs = slice(hh * PB, (hh + 1) * PB)
                    m = PO.do(lambda e, hs=hs, hh=hh: e.tensor_tensor(
                        y[:, :, hs], y[:, :, hs], spread(fb["elo"][:, hh * NC:(hh + 1) * NC], PB), ALU.mult), m)
                m = PO.do(lambda e, ws=ws: e.tensor_tensor(y[:, :, ws], y[:, :, ws], Dx[:, :, ws], ALU.add), m)
                m_yb.append(m)
        m_sq = []
        for c in range(NC):
            m = AC.do(lambda e, c=c: e.activation(U[:, c, :], y[:, c, :], ACT.Square, accum_out=ssq[:, c:c + 1]),
                      m_yb, PE.last())
        m = PO.do(lambda e: e.tensor_scalar(rms, ssq, 1.0 / WB, None, ALU.mult), m)
        m = PO.do(lambda e: e.tensor_scalar(rms, rms, 1e-5, None, ALU.add), m)
        m_rms = PO.do(lambda e: e.tensor_tensor(rms, rms, neghalf[:, 0:NC], ALU.pow), m)
        m_gt = []
        m_x2 = []
        for q in range(2):
            for i in range(XT):
                bank, free, users = work.take()
                for c in range(4 * q, 4 * q + 4):
                    m = PE.do(lambda e, c=c, i=i, bank=bank: e.transpose(bank[:, (c % 4) * P:(c % 4 + 1) * P],
                                                                         y[:, c, i * P:(i + 1) * P], ident[:, :]),
                              m_yb, free)
                ts = slice(q * BANK, (q + 1) * BANK)
                m = DV.do(lambda e, i=i, ts=ts, bank=bank: e.scalar_tensor_tensor(
                    out=xt[:, i, ts], in0=bank, scalar=nw[:, i:i + 1], in1=zc[:, i, ts], op0=ALU.mult, op1=ALU.mult),
                    m, m_z, m_nw, m_u)
                users.append(m)
                m_gt.append(m)
            for c2 in (4 * q, 4 * q + 2):
                bank, free, users = work.take()
                for c in (c2, c2 + 1):
                    for i in range(XT):
                        m = PE.do(lambda e, c=c, i=i, bank=bank: e.matmul(
                            bank[:, (c % 2) * D:(c % 2 + 1) * D], xt[:, i, c * P:(c + 1) * P], wout[:, i, :],
                            start=(i == 0), stop=(i == XT - 1)), m_gt, m_wout, free)
                for c in (c2, c2 + 1):
                    m_c = DV.do(lambda e, c=c, bank=bank: e.scalar_tensor_tensor(
                        out=x[:, c, :], in0=bank[:, (c % 2) * D:(c % 2 + 1) * D], scalar=rms[:, c:c + 1],
                        in1=x[:, c, :], op0=ALU.mult, op1=ALU.add), m, m_rms)
                    m_x2.append(m_c)
                users.append(m_c)
        join()

        m_x3 = experts(1, m_x2)
        m_out = [SP.copy(stream(f"x{c}"), io["out"][c * P:(c + 1) * P, :], x[:, c, :], m_x3[c]) for c in range(NC)]
        SP.wait(m_out)


def kernel(**inputs):
    import concourse.bacc as bacc
    from concourse.bass_utils import run_bass_kernel_spmd

    a = {n: np.ascontiguousarray(np.asarray(t)) for n, t in inputs.items()}

    def k_major(w):
        return w.reshape(KD, P, -1).transpose(1, 0, 2)

    win = a["L0_attn_a_Win"]
    wx, wz = win[:HA * PA], win[HA * PA:2 * HA * PA]
    wb, wc = (win[2 * HA * PA + i * HA * NS:2 * HA * PA + (i + 1) * HA * NS].reshape(PAIRS, 2, NS, D) for i in range(2))
    w_a = np.stack([wx.reshape(PAIRS, P, D), wb[:, 0], wb[:, 1], wc[:, 0], wc[:, 1], wz.reshape(PAIRS, P, D)], 1)
    w_a = w_a.reshape(PAIRS, 6, P, KD, P).transpose(0, 4, 3, 1, 2)
    cb_, cc_ = (a[f"L0_attn_a_conv_w_{n}"].reshape(PAIRS, 2, NS, TAPS) for n in "bc")
    cx_ = a["L0_attn_a_conv_w_x"].reshape(PAIRS, P, TAPS)
    conv_a = np.stack([cx_, cb_[:, 0], cb_[:, 1], cc_[:, 0], cc_[:, 1]], 1).transpose(2, 0, 1, 3)
    wib = a["L0_attn_b_in_proj_w"]
    order = [wib[:, 2 * WB:2 * WB + NS], wib[:, 2 * WB + NS:2 * WB + 2 * NS]]
    order += [wib[:, WB + i * P:WB + (i + 1) * P] for i in range(XT)] + [wib[:, i * P:(i + 1) * P] for i in range(XT)]
    cwb, cbb = a["L0_attn_b_conv_w"], a["L0_attn_b_conv_b"]
    tiles_b = [slice(WB, WB + NS), slice(WB + NS, WB + 2 * NS)] + [slice(i * P, (i + 1) * P) for i in range(XT)]
    f = {n: a[f"L0_ffn_{n}"] for n in ("wa", "rg", "rgb", "rw1", "rb1", "rw2", "rb2", "sg", "sgb", "sw1", "sb1",
                                       "sw2", "sb2")}

    def up(routed, shared):
        return np.concatenate([routed, shared]).reshape(EXPERTS, KD, P, F).transpose(0, 2, 1, 3)

    arrays = {
        "x": a["L0_attn_a_x"].reshape(T, D),
        "w_a": w_a,
        "wdt_a": k_major(win[-HA:].T),
        "conv_a": conv_a,
        "dtb_a": a["L0_attn_a_dt_bias"].reshape(1, HA),
        "alog_a": a["L0_attn_a_A_log"].reshape(1, HA),
        "wout_a": a["L0_attn_a_Wout"].T.reshape(PAIRS // GROUP, GROUP, P, D).transpose(0, 2, 1, 3),
        "w_b": np.stack([k_major(w) for w in order]),
        "wdt_b": k_major(wib[:, -HB:]),
        "conv_b": np.stack([cwb[s] for s in tiles_b], 1),
        "convbias_b": np.stack([cbb[s] for s in tiles_b], 1),
        "norm_b": a["L0_attn_b_norm_w"].reshape(XT, P).T,
        "dtb_b": a["L0_attn_b_dt_bias"].reshape(1, HB),
        "alog_b": a["L0_attn_b_A_log"].reshape(1, HB),
        "d_b": a["L0_attn_b_D"].reshape(1, HB),
        "wout_b": a["L0_attn_b_out_proj_w"].reshape(XT, P, D).transpose(1, 0, 2),
        "wa_e": k_major(f["wa"]),
        "wg": up(f["rg"], f["sg"]),
        "wu": up(f["rw1"], f["sw1"]),
        "wd": np.concatenate([f["rw2"], f["sw2"]]),
        "gb": np.concatenate([f["rgb"], f["sgb"]]).T,
        "ub": np.concatenate([f["rb1"], f["sb1"]]).T,
        "b2": np.concatenate([f["rb2"], f["sb2"]]),
        "ident": np.eye(P, dtype=np.float32),
        "tri": np.triu(np.ones((P, P), np.float32)),
        "revidx": (E - np.arange(E, dtype=np.float32)).reshape(1, E),
    }
    arrays = {n: np.ascontiguousarray(t) for n, t in arrays.items()}
    nc = bacc.Bacc("TRN2", target_bir_lowering=False, num_devices=1)
    io = {n: nc.dram_tensor(f"in_{n}", t.shape, F32, kind="ExternalInput").ap() for n, t in arrays.items()}
    io["out"] = nc.dram_tensor("out", (T, D), F32, kind="ExternalOutput").ap()
    hybrid_block(nc, io)
    r = run_bass_kernel_spmd(nc, [{f"in_{n}": t for n, t in arrays.items()}], core_ids=[0])
    return r.results[0]["out"].reshape(1, T, D)
```

```python
from contextlib import ExitStack

import numpy as np

import concourse.bass as bass
from concourse import mybir
from concourse.alu_op_type import AluOpType as ALU

ACT = mybir.ActivationFunctionType
F32 = mybir.dt.float32
AX_X = mybir.AxisListType.X

P = 128
T, D = 1024, 256
NC = T // P
KD = D // P
TAPS = 4
NS = 128
BANK = 512

HA, PA = 32, 64
PAIRS = HA * PA // P
GROUP = 4
HB, PB = 64, 8
WB = HB * PB
XT = WB // P
QUAD = 32
SUBS = QUAD // PB

E, F, SH = 16, 128, 2
EXPERTS = E + SH

ARENA = 30000
DECAY_FLOOR = -105.0
QUANTUM = 1.5 * 2.0 ** 13
MASKED = -30000.0


class Mark:

    def __init__(self, sem, value):
        self.sem, self.value = sem, value


class Lane:

    def __init__(self, engine, sem):
        self.engine, self.sem, self.count, self.reached = engine, sem, 0, {}

    def wait(self, *marks):
        for m in flat(marks):
            if m.value > self.reached.get(m.sem.name, 0):
                self.engine.wait_ge(m.sem, m.value)
                self.reached[m.sem.name] = m.value

    def do(self, build, *after, mark=True):
        self.wait(*after)
        instruction = build(self.engine)
        if mark:
            instruction.then_inc(self.sem, 1)
            self.count += 1
        return self.last()

    def last(self):
        return Mark(self.sem, self.count)

    def then(self, build, *after):
        return self.do(build, self.last(), *after)

    def copy(self, stream, dst, src, *after):
        self.wait(*after)
        self.engine.dma_start(dst, src).then_inc(stream.sem, 16)
        stream.count += 16
        return Mark(stream.sem, stream.count)


def flat(marks):
    out = []
    for m in marks:
        out += flat(m) if isinstance(m, (list, tuple)) else [m]
    return [m for m in out if m is not None]


class Stream:

    def __init__(self, sem):
        self.sem, self.count = sem, 0


class Ring:

    def __init__(self, buffers):
        self.buffers, self.users, self.n = buffers, [[] for _ in buffers], 0

    def take(self):
        i = self.n % len(self.buffers)
        self.n += 1
        before, self.users[i] = self.users[i], []
        return self.buffers[i], before, self.users[i]


def spread(ap, n):
    return ap.unsqueeze(len(ap.shape)).to_broadcast([*ap.shape, n])


def hybrid_block(nc, io):
    with ExitStack() as ctx:
        def sb(name, shape):
            return ctx.enter_context(nc.sbuf_tensor(name, shape, F32))

        def sem(name):
            return ctx.enter_context(nc.semaphore(name))

        PE, AC, DV, PO, SP = (Lane(engine, sem(f"{name}_done")) for name, engine in (
            ("pe", nc.tensor), ("act", nc.scalar), ("dve", nc.vector), ("pool", nc.gpsimd), ("sp", nc.sync)))

        x = sb("x", [P, NC, D])
        v = sb("v", [P, NC, D])
        vT = sb("vT", [P, KD, T])
        ident = sb("ident", [P, P])
        tri = sb("tri", [P, P])
        ones = sb("ones", [P, P])
        revidx = sb("revidx", [P, E])
        neghalf = sb("neghalf", [P, 2 * NC])
        bn6 = sb("bn6", [P, NC, 6])
        bn2 = sb("bn2", [P, NC, 2])
        rstd = sb("rstd", [P, NC])
        eps_rstd = sb("eps_rstd", [P, NC])
        bcast = [sb(f"bcast{i}", [P, T])[:, :] for i in range(4)]
        small = sb("small", [P, 13, 512])
        arena = sb("arena", [P, ARENA])
        psum = ctx.enter_context(nc.psum_tensor("psum", [P, 8 * BANK], F32))
        wide = Ring([psum[:, 2 * i * BANK:(2 * i + 2) * BANK] for i in range(2)])
        work = Ring([psum[:, i * BANK:(i + 1) * BANK] for i in range(4, 8)])

        scratch_a = nc.dram_tensor("scratch_a", [HA, T], F32).ap()
        scratch_b = nc.dram_tensor("scratch_b", [HB, T], F32).ap()
        scratch_e = [nc.dram_tensor(f"scratch_e{i}", [E, T], F32).ap() for i in range(2)]

        streams = {}

        def stream(name):
            if name not in streams:
                streams[name] = Stream(sem(f"dma_{name}"))
            return streams[name]

        bcast_ring = Ring(list(range(len(bcast))))

        def load_rows(row, *after):
            i, before, users = bcast_ring.take()
            m = SP.copy(stream(f"bcast{i}"), bcast[i], row.to_broadcast([P, T]), before, *after)
            return bcast[i], m, users

        def join():
            marks = [L.last() for L in (PE, AC, DV, PO)] + [Mark(s.sem, s.count) for s in streams.values()]
            for L in (PE, AC, DV, PO, SP):
                L.wait(marks)

        m_x = [SP.copy(stream(f"x{c}"), x[:, c, :], io["x"][c * P:(c + 1) * P, :]) for c in range(NC)]
        m_ident = SP.copy(stream("ident"), ident[:, :], io["ident"])
        m_tri = SP.copy(stream("tri"), tri[:, :], io["tri"])
        m_rev = SP.copy(stream("rev"), revidx[:, :], io["revidx"].to_broadcast([P, E]))
        m_ones = PO.do(lambda e: e.memset(ones[:, :], 1.0))
        m_half = PO.do(lambda e: e.memset(neghalf[:, :], -0.5))

        def layer_norm(m_in, before):
            done = []
            for c in range(NC):
                m = DV.do(lambda e, c=c: e.bn_stats(bn6[:, c, :], x[:, c, :]), m_in[c], before)
                m = DV.do(lambda e, c=c: e.bn_aggr(bn2[:, c, :], bn6[:, c, :]), m)
                m = PO.do(lambda e, c=c: e.tensor_scalar(eps_rstd[:, c:c + 1], bn2[:, c, 1:2], 1e-5, None, ALU.add), m)
                m = PO.do(lambda e, c=c: e.tensor_tensor(rstd[:, c:c + 1], eps_rstd[:, c:c + 1],
                                                         neghalf[:, 0:1], ALU.pow), m, m_half)
                m_v = DV.do(lambda e, c=c: e.tensor_scalar(v[:, c, :], x[:, c, :], bn2[:, c, 0:1], rstd[:, c:c + 1],
                                                           ALU.subtract, ALU.mult), m)
                if c % 2 == 0:
                    bank, free, users = work.take()
                for k in range(KD):
                    o = bank[:, ((c % 2) * KD + k) * P:((c % 2) * KD + k + 1) * P]
                    m = PE.do(lambda e, c=c, k=k, o=o: e.transpose(o, v[:, c, k * P:(k + 1) * P], ident[:, :]),
                              m_v, m_ident, free)
                if c % 2 == 1:
                    m = AC.do(lambda e, c=c, bank=bank: e.copy(
                        vT[:, :, (c - 1) * P:(c + 1) * P].rearrange("p k (c t) -> p c k t", c=2),
                        bank.rearrange("p (c k t) -> p c k t", c=2, k=KD)), m, before)
                    users.append(m)
                    done += [m]
            return [m_v], done

        def softplus(raw, n, dst, tmp, m):
            pos, e_, u, l = (tmp[i][:, 0:n] for i in range(4))
            DV.then(lambda e: e.tensor_scalar(pos, raw, 0.0, None, ALU.max), m)
            m = DV.then(lambda e: e.scalar_tensor_tensor(out=e_, in0=pos, scalar=-2.0, in1=raw, op0=ALU.mult, op1=ALU.add))
            m = AC.do(lambda e: e.activation(e_, e_, ACT.Exp), m)
            m = DV.do(lambda e: e.tensor_scalar(u, e_, 1.0, None, ALU.add), m)
            m_l = AC.do(lambda e: e.activation(l, u, ACT.Ln), m)
            DV.then(lambda e: e.scalar_tensor_tensor(out=e_, in0=u, scalar=-1.0, in1=e_, op0=ALU.add, op1=ALU.subtract))
            DV.then(lambda e: e.tensor_tensor(pos, pos, l, ALU.add), m_l)
            DV.then(lambda e: e.reciprocal(u, u), m_l)
            DV.then(lambda e: e.tensor_tensor(u, u, e_, ALU.mult))
            return DV.then(lambda e: e.tensor_tensor(dst, pos, u, ALU.subtract))

        def decays(H, raw, m_raw, a_log, m_alog, scratch):
            n = H * NC
            f = {}
            for i, name in enumerate(("dt", "t0", "t1", "t2", "t3", "hi", "lo", "cumhi", "cumlo", "tothi",
                                      "totlo", "wd", "dec")):
                f[name] = small[:, i, 0:n]
            m = softplus(raw, n, f["dt"], [small[:, i, :] for i in range(1, 5)], m_raw)
            a = f["t0"]
            m_ea = AC.do(lambda e: e.activation(a_log, a_log, ACT.Exp), m_alog)
            DV.then(lambda e: e.scalar_tensor_tensor(out=a.rearrange("p (h c) -> p h c", c=NC),
                                                     in0=f["dt"].rearrange("p (h c) -> p h c", c=NC), scalar=-1.0,
                                                     in1=spread(a_log, NC), op0=ALU.mult, op1=ALU.mult), m_ea)
            DV.then(lambda e: e.tensor_scalar(a, a, DECAY_FLOOR, None, ALU.max))
            DV.then(lambda e: e.tensor_scalar(f["hi"], a, QUANTUM, None, ALU.add))
            DV.then(lambda e: e.tensor_scalar(f["hi"], f["hi"], QUANTUM, None, ALU.subtract))
            m = DV.then(lambda e: e.tensor_tensor(f["lo"], a, f["hi"], ALU.subtract))
            for lhs, m_lhs, src, dst in ((tri, m_tri, "hi", "cumhi"), (tri, m_tri, "lo", "cumlo"),
                                         (ones, m_ones, "hi", "tothi"), (ones, m_ones, "lo", "totlo")):
                bank, free, users = work.take()
                mp = PE.do(lambda e, lhs=lhs, src=src, bank=bank: e.matmul(bank[:, 0:n], lhs[:, :], f[src],
                                                                           start=True, stop=True), m, m_lhs, free)
                m_c = DV.do(lambda e, dst=dst, bank=bank: e.tensor_copy(f[dst], bank[:, 0:n]), mp)
                users.append(m_c)
                if dst == "cumhi":
                    bank, free, users = work.take()
                    for q in range(n // P):
                        mp = PE.do(lambda e, q=q, bank=bank: e.transpose(
                            bank[:, q * P:(q + 1) * P], f["cumhi"][:, q * P:(q + 1) * P], ident[:, :]), m_c, m_ident, free)
                    rows = f["t1"]
                    m_r = DV.do(lambda e, bank=bank: e.tensor_copy(rows, bank[:, 0:n]), mp)
                    users.append(m_r)
                    m_scr = SP.copy(stream("scratch"), scratch.rearrange("(q g) (c t) -> (g c) q t", q=n // P, c=NC),
                                    rows.rearrange("p (q t) -> p q t", t=P), m_r)
            AC.do(lambda e: e.activation(f["t2"], f["cumlo"], ACT.Exp), DV.last())
            m = AC.do(lambda e: e.activation(f["t3"], f["cumlo"], ACT.Exp, scale=-1.0))
            f["elo"], f["ehi"] = f["t2"], f["t0"]
            m_dtl = DV.then(lambda e: e.tensor_tensor(f["t3"], f["t3"], f["dt"], ALU.mult), m)
            f["dtl"] = f["t3"]
            AC.do(lambda e: e.activation(f["ehi"], f["cumhi"], ACT.Exp))
            DV.then(lambda e: e.tensor_tensor(f["wd"], f["tothi"], f["cumhi"], ALU.subtract))
            DV.then(lambda e: e.tensor_tensor(f["wd"], f["wd"], f["totlo"], ALU.add))
            m = DV.then(lambda e: e.tensor_tensor(f["dec"], f["tothi"], f["totlo"], ALU.add))
            AC.do(lambda e: e.activation(f["wd"], f["wd"], ACT.Exp), m)
            m = AC.do(lambda e: e.activation(f["dec"], f["dec"], ACT.Exp))
            return f, [m, m_dtl], m_scr

        def conv(tile_out, bank, m_pe, w, m_w, free, users, marks, bias=None):
            m = AC.do(lambda e: e.activation(tile_out, bank, ACT.Identity, scale=w[:, TAPS - 1:TAPS],
                                             bias=0.0 if bias is None else bias), m_pe, m_w, free)
            for s in range(1, TAPS):
                yield
                m = DV.do(lambda e, s=s: e.scalar_tensor_tensor(
                    out=tile_out[:, s:T], in0=bank[:, 0:T - s], scalar=w[:, TAPS - 1 - s:TAPS - s],
                    in1=tile_out[:, s:T], op0=ALU.mult, op1=ALU.add), m, m_w)
            users.append(m)
            yield
            marks.append(AC.do(lambda e: e.activation(tile_out, tile_out, ACT.Silu), m))

        def project(weight, m_w, m_vT):
            bank, free, users = wide.take()
            for half in range(2):
                for k in range(KD):
                    m = PE.do(lambda e, k=k, half=half: e.matmul(
                        bank[:, half * BANK:(half + 1) * BANK], weight(k), vT[:, k, half * BANK:(half + 1) * BANK],
                        start=(k == 0), stop=(k == KD - 1)), m_w, m_vT, free, mark=(half == 1 and k == KD - 1))
            return bank, m, users

        def decay_matrix(rows, m_rows, cum, m_cum, on_vector):
            r3 = rows[:, :].rearrange("p (c t) -> p c t", t=P)
            lane = DV if on_vector else PO
            m = lane.do(lambda e: e.tensor_tensor(r3, r3, spread(cum, P), ALU.subtract), m_rows, m_cum)
            m = PO.do(lambda e: e.affine_select(out=r3, in_=r3, compare_op=ALU.is_ge, fill=MASKED, base=0,
                                                pattern=[[0, NC], [1, P]], channel_multiplier=-1), m)
            return AC.do(lambda e: e.activation(rows[:, :], rows[:, :], ACT.Exp), m)

        class Arena:
            def __init__(self):
                self.at = 0

            def __call__(self, n):
                self.at += n
                assert self.at <= ARENA, self.at
                return arena[:, self.at - n:self.at]

        A = Arena()
        TILES = 6
        CONV = TILES - 1
        w_ring = Ring([A(KD * TILES * P).rearrange("p (k i m) -> p k i m", k=KD, i=TILES) for _ in range(2)])
        cv_ring = Ring([A(CONV * T).rearrange("p (i t) -> p i t", i=CONV) for _ in range(2)])
        z_ring = Ring([A(T) for _ in range(3)])
        cw = A(PAIRS * 5 * TAPS).rearrange("p (j i k) -> p j i k", i=5, k=TAPS)
        wdt = A(KD * HA).rearrange("p (k h) -> p k h", k=KD)
        dtb, alog = A(HA), A(HA)
        raw_a = A(HA * NC)
        u_ring = Ring([(A(T).rearrange("p (c m) -> p c m", c=NC), A(T).rearrange("p (c m) -> p c m", c=NC))])
        bt_ring = Ring([A(T) for _ in range(2)])
        st_ring = Ring([A(NC * PA).rearrange("p (c m) -> p c m", c=NC) for _ in range(2)])
        y_ring = Ring([A(T).rearrange("p (c m) -> p c m", c=NC)])
        y2 = A(T)
        elo2 = A(HA * NC)
        gated = Ring([A(GROUP * T).rearrange("p (g t) -> p g t", g=GROUP)])
        wout_ring = Ring([A(GROUP * D).rearrange("p (g d) -> p g d", g=GROUP)])
        nrm = [A(2 * NC) for _ in range(2)]

        m_cw = SP.copy(stream("cw"), cw, io["conv_a"])
        m_wdt = SP.copy(stream("wdt"), wdt, io["wdt_a"])
        m_dtb = SP.copy(stream("dtb"), dtb, io["dtb_a"].to_broadcast([P, HA]))
        m_alog = SP.copy(stream("alog"), alog, io["alog_a"].to_broadcast([P, HA]))
        wq = {}

        def load_pair(j):
            w, before, users = w_ring.take()
            wq[j] = (w, SP.copy(stream(f"wa{j % 2}"), w, io["w_a"][j], before), users)

        load_pair(0)
        load_pair(1)
        m_zero = [PO.do(lambda e, b=b: e.memset(b[:, 0, :], 0.0)) for b in st_ring.buffers]

        _, m_vT = layer_norm(m_x, None)

        def project_dt(wdt, m_wdt, H, bias, m_bias, raw):
            bank, free, users = work.take()
            for c in range(NC):
                for k in range(KD):
                    m = PE.do(lambda e, c=c, k=k: e.matmul(bank[:, c * H:(c + 1) * H], vT[:, k, c * P:(c + 1) * P],
                                                           wdt[:, k, :], start=(k == 0), stop=(k == KD - 1)),
                              m_vT[c // 2], m_wdt, free, mark=(c == NC - 1))
            m = DV.do(lambda e: e.tensor_tensor(raw.rearrange("p (h c) -> p h c", c=NC),
                                                bank[:, 0:H * NC].rearrange("p (c h) -> p h c", c=NC),
                                                spread(bias, NC), ALU.add), m, m_bias)
            users.append(m)
            return m

        m = project_dt(wdt, m_wdt, HA, dtb, m_dtb, raw_a)
        fa, m_fa, m_scr = decays(HA, raw_a, m, alog, m_alog, scratch_a)
        m = DV.then(lambda e: e.tensor_tensor(elo2, fa["elo"], fa["elo"], ALU.mult), m_fa)
        m_fa = [m_fa, DV.then(lambda e: e.tensor_scalar(elo2, elo2, 1.0 / PA, None, ALU.mult))]

        def fac(name, h):
            return fa[name][:, h * NC:(h + 1) * NC]

        conv_out, z_out, rows, heads_y, group = {}, {}, {}, {}, {}

        def project_pair(j):
            w, m_w, w_users = wq.pop(j)
            out, free, users = cv_ring.take()
            zt, z_free, z_users = z_ring.take()
            marks = []
            conv_out[j] = (out, marks, users)
            for i in range(CONV):
                bank, m, b_users = project(lambda k, i=i: w[:, k, i, :], m_w, m_vT)
                yield from conv(out[:, i, :], bank, m, cw[:, j, i, :], m_cw, free, b_users, marks)
                yield
            bank, m, b_users = project(lambda k: w[:, k, CONV, :], m_w, m_vT)
            w_users.append(m)
            yield
            m = AC.do(lambda e: e.activation(zt, bank, ACT.Silu), m, z_free)
            b_users.append(m)
            z_out[j] = (zt, m, z_users)
            if j + 2 < PAIRS:
                load_pair(j + 2)
            yield

        PROJECT_STEPS = 5 * CONV + 2

        def load_decays(j):
            for h in (2 * j, 2 * j + 1):
                rows[h] = load_rows(scratch_a[h:h + 1, :], m_scr)

        def decay_pair(j):
            for h in (2 * j, 2 * j + 1):
                buf, m, users = rows[h]
                rows[h] = (buf, decay_matrix(buf, m, fac("cumhi", h), m_fa, False), users)

        def unit(columns, n, after, evacuate):
            bank, free, users = work.take()
            for i in range(n):
                m = PE.do(columns(bank, i), after, free, mark=(i == n - 1))
            m = evacuate(bank, m)
            users.append(m)
            return m

        def transposes(src):
            return lambda bank, i: lambda e: e.transpose(bank[:, i * P:(i + 1) * P], src(i), ident[:, :])

        def chunk(ap, c):
            return ap[:, c * P:(c + 1) * P]

        def scan_pair(j):
            out, m_cv, cv_users = conv_out.pop(j)
            (U, Ud), u_free, u_users = u_ring.take()
            m_u = []

            def scale_u(q):
                cs = slice(4 * q, 4 * q + 4)

                def evacuate(bank, m):
                    src = bank.rearrange("p (c m) -> p c m", c=4)
                    for g in range(2):
                        sl = slice(g * PA, (g + 1) * PA)
                        m = DV.do(lambda e: e.tensor_tensor(U[:, cs, sl], src[:, :, sl],
                                                            spread(fac("dtl", 2 * j + g)[:, cs], PA), ALU.mult),
                                  m, m_fa, u_free)
                    return m
                m = unit(transposes(lambda i: chunk(out[:, 0, :], 4 * q + i)), 4, [m_cv[0], m_ident], evacuate)
                for g in range(2):
                    sl = slice(g * PA, (g + 1) * PA)
                    m = PO.do(lambda e: e.tensor_tensor(Ud[:, cs, sl], U[:, cs, sl],
                                                        spread(fac("wd", 2 * j + g)[:, cs], PA), ALU.mult), m, m_fa, u_free)
                m_u.append(m)

            y, y_free, y_users = y_ring.take()
            head = [{}, {}]

            def turn_b(g, q):
                s = head[g]
                if q == 0:
                    s["bt"], s["bt_free"], s["bt_users"] = bt_ring.take()
                    s["m_bt"] = []
                s["m_bt"].append(unit(
                    transposes(lambda i: chunk(out[:, 1 + g, :], 4 * q + i)), 4, [m_cv[1 + g], m_ident],
                    lambda bank, m: AC.do(lambda e: e.copy(s["bt"][:, q * BANK:(q + 1) * BANK], bank), m, s["bt_free"])))

            def mix(g, q):
                s = head[g]
                buf, m_e, _ = rows[2 * j + g]
                half = buf[:, q * BANK:(q + 1) * BANK]
                s.setdefault("m_m", []).append(unit(
                    lambda bank, i: lambda e: e.matmul(chunk(bank, i), chunk(out[:, 1 + g, :], 4 * q + i),
                                                       chunk(out[:, 3 + g, :], 4 * q + i), start=True, stop=True),
                    4, [m_cv[1 + g], m_cv[3 + g]],
                    lambda bank, m: DV.do(lambda e: e.tensor_tensor(half, bank, half, ALU.mult), m, m_e)))

            def states(g):
                s = head[g]
                hs = slice(g * PA, (g + 1) * PA)
                s["st"], st_free, s["st_users"] = st_ring.take()
                st = s["st"]

                def chain(bank, m):
                    for c in range(NC - 1):
                        m = DV.do(lambda e: e.scalar_tensor_tensor(
                            out=st[:, c + 1, :], in0=st[:, c, :], scalar=fac("dec", 2 * j + g)[:, c:c + 1],
                            in1=bank[:, c * PA:(c + 1) * PA], op0=ALU.mult, op1=ALU.add), m, m_fa, st_free, m_zero)
                    return m
                s["m_st"] = unit(lambda bank, c: lambda e: e.matmul(bank[:, c * PA:(c + 1) * PA], chunk(s["bt"], c),
                                                                    Ud[:, c, hs], start=True, stop=True),
                                 NC - 1, [s["m_bt"], m_u], chain)
                s["bt_users"].append(PE.last())

            def outputs(g):
                s = head[g]
                hs = slice(g * PA, (g + 1) * PA)
                bank_i, free, users_i = work.take()
                buf, _, e_users = rows.pop(2 * j + g)
                for c in range(NC):
                    m_i = PE.do(lambda e: e.matmul(bank_i[:, c * PA:(c + 1) * PA], chunk(buf, c), U[:, c, hs],
                                                   start=True, stop=True), s["m_m"], m_u, free, mark=(c == NC - 1))
                e_users.append(m_i)
                yield
                m = unit(lambda bank, c: lambda e: e.matmul(bank[:, c * PA:(c + 1) * PA], chunk(out[:, 3 + g, :], c),
                                                            s["st"][:, c, :], start=True, stop=True),
                         NC, [s["m_st"]],
                         lambda bank, m: DV.do(lambda e: e.tensor_tensor(
                             y[:, :, hs], bank.rearrange("p (c m) -> p c m", c=NC), spread(fac("ehi", 2 * j + g), PA),
                             ALU.mult), m, y_free))
                s["st_users"].append(PE.last())
                yield
                m = DV.do(lambda e: e.tensor_tensor(y[:, :, hs], bank_i.rearrange("p (c m) -> p c m", c=NC),
                                                    y[:, :, hs], ALU.add), m, m_i)
                users_i.append(m)
                s["m_y"] = m
                yield

            scale_u(0)
            yield
            scale_u(1)
            yield
            turn_b(0, 0)
            yield
            turn_b(0, 1)
            yield
            yield from finish_pair(j - 1)
            mix(0, 0)
            yield
            mix(0, 1)
            yield
            states(0)
            yield
            turn_b(1, 0)
            yield
            turn_b(1, 1)
            yield
            mix(1, 0)
            yield
            mix(1, 1)
            yield
            states(1)
            yield
            yield from outputs(0)
            yield from outputs(1)
            u_users.append(PE.last())
            cv_users.append(PE.last())
            y2v = y2.rearrange("p (c m) -> p c m", c=NC)
            m_y = [head[0]["m_y"], head[1]["m_y"]]
            m = PO.do(lambda e: e.tensor_tensor(y2v, y, y, ALU.mult), m_y, y2_users)
            yield
            m = DV.do(lambda e: e.tensor_reduce(nrm[0].rearrange("p (g c) -> p g c", g=2),
                                                y2.rearrange("p (c g m) -> p g c m", c=NC, g=2), AX_X, ALU.add), m,
                      nrm_users)
            y2_users[:] = [m]
            pr = slice(2 * j * NC, (2 * j + 2) * NC)
            m = PO.do(lambda e: e.tensor_tensor(nrm[1], nrm[0], elo2[:, pr], ALU.mult), m)
            nrm_users[:] = [m]
            m = PO.do(lambda e: e.tensor_scalar(nrm[1], nrm[1], 1e-6, None, ALU.add), m)
            m = PO.do(lambda e: e.tensor_tensor(nrm[1], nrm[1], neghalf[:, 0:2 * NC], ALU.pow), m)
            m = PO.do(lambda e: e.tensor_tensor(nrm[1], nrm[1], fa["elo"][:, pr], ALU.mult), m)
            for g in range(2):
                hs = slice(g * PA, (g + 1) * PA)
                m = PO.do(lambda e: e.tensor_tensor(y[:, :, hs], y[:, :, hs],
                                                    spread(nrm[1][:, g * NC:(g + 1) * NC], PA), ALU.mult), m)
            heads_y[j] = (y, m, y_users)
            yield

        y2_users, nrm_users = [], []
        m_xa = [None] * (NC // 2)

        def finish_pair(j):
            if j < 0:
                return
            y, m_y, y_users = heads_y.pop(j)
            zt, m_z, z_users = z_out.pop(j)
            if j % GROUP == 0:
                gt, g_free, g_users = gated.take()
                wo, w_free, w_users = wout_ring.take()
                m_wo = SP.copy(stream("wo"), wo, io["wout_a"][j // GROUP], w_free)
                group.update(gt=gt, free=g_free, users=g_users, wo=wo, m_wo=m_wo, w_users=w_users, m=[])
            gt, wo = group["gt"], group["wo"]
            for q in range(2):
                ts = slice(q * BANK, (q + 1) * BANK)
                m = unit(transposes(lambda i: y[:, 4 * q + i, :]), 4, [m_y, m_ident],
                         lambda bank, m: DV.do(lambda e: e.tensor_tensor(gt[:, j % GROUP, ts], bank, zt[:, ts], ALU.mult),
                                               m, m_z, group["free"]))
                group["m"].append(m)
                yield
            y_users.append(PE.last())
            z_users.append(m)
            if j % GROUP == GROUP - 1:
                for q in range(NC // 2):
                    def products(bank, i):
                        c, g = 2 * q + i // GROUP, i % GROUP
                        return lambda e: e.matmul(bank[:, (c % 2) * D:(c % 2 + 1) * D], gt[:, g, c * P:(c + 1) * P],
                                                  wo[:, g, :], start=(g == 0), stop=(g == GROUP - 1))
                    xs = x[:, 2 * q:2 * q + 2, :]
                    m_xa[q] = unit(products, 2 * GROUP, [group["m"], group["m_wo"]],
                                   lambda bank, m: DV.do(lambda e: e.tensor_tensor(
                                       xs, bank.rearrange("p (c d) -> p c d", c=2), xs, ALU.add), m, m_xa[q]))
                    yield
                group["users"].append(PE.last())
                group["w_users"].append(PE.last())

        SCAN_STEPS = 24

        def interleave(first, n_first, second, n_second):
            done = [0, 0]
            live = [first, second]
            while any(live):
                rate = [done[0] / n_first if live[0] else 9e9, done[1] / n_second if live[1] else 9e9]
                i = 0 if rate[0] <= rate[1] else 1
                if next(live[i], live) is live:
                    live[i] = None
                done[i] += 1

        def pair_steps(j):
            if j + 1 < PAIRS:
                load_decays(j + 1)
            for n, _ in enumerate(scan_pair(j)):
                if n == 8 and j + 1 < PAIRS:
                    decay_pair(j + 1)
                yield

        load_decays(0)
        decay_pair(0)
        for _ in project_pair(0):
            pass
        for j in range(PAIRS):
            interleave(pair_steps(j), SCAN_STEPS, project_pair(j + 1) if j + 1 < PAIRS else None, PROJECT_STEPS)
        for _ in finish_pair(PAIRS - 1):
            pass
        m_xa = [m_xa[c // 2] for c in range(NC)]
        join()

        def experts(n, m_in):
            G = Arena()
            wg_ring = Ring([tuple(G(KD * F).rearrange("p (k f) -> p k f", k=KD) for _ in range(2)) + (G(D),)
                            for _ in range(4)])
            wa = G(KD * E).rearrange("p (k e) -> p k e", k=KD)
            gb, ub = G(EXPERTS), G(EXPERTS)
            aff, key, one, comb, c2 = (G(NC * E).rearrange("p (e c) -> p e c", c=NC) for _ in range(5))
            m1, m2, km, den = (G(NC) for _ in range(4))
            combT = G(T)
            b2w = G(D)
            gate_ring = Ring([G(BANK) for _ in range(3)])
            hid_ring = Ring([G(BANK) for _ in range(3)])
            wq = {}
            order = list(range(E, EXPERTS)) + list(range(E))

            def load_expert(p):
                i = order[p]
                w, before, users = wg_ring.take()
                got = []
                for part, name in zip(w, ("wg", "wu", "wd")):
                    m = SP.copy(stream(f"{name}{p % 4}"), part, io[name][i], before)
                    got.append(m)
                wq[i] = (w, got, users)

            m_wa = SP.copy(stream("wa_e"), wa, io["wa_e"])
            m_gb = SP.copy(stream("gb"), gb, io["gb"])
            m_ub = SP.copy(stream("ub"), ub, io["ub"])
            m_b2 = SP.copy(stream("b2"), b2w[0:EXPERTS, :], io["b2"])
            for i in range(3):
                load_expert(i)
            m_v, m_vT = layer_norm(m_in, None)

            bank, free, users = work.take()
            for c in range(NC):
                for k in range(KD):
                    m = PE.do(lambda e, c=c, k=k: e.matmul(bank[:, c * E:(c + 1) * E], vT[:, k, c * P:(c + 1) * P],
                                                           wa[:, k, :], start=(k == 0), stop=(k == KD - 1)),
                              m_vT[c // 2], m_wa, free, mark=(c == NC - 1))
            m = AC.do(lambda e: e.activation(aff, bank[:, 0:NC * E].rearrange("p (c e) -> p e c", c=NC), ACT.Exp,
                                             scale=-1.0), m)
            users.append(m)
            DV.do(lambda e: e.tensor_scalar(aff, aff, 1.0, None, ALU.add), m)
            DV.then(lambda e: e.reciprocal(aff, aff))

            def by_chunk(ap):
                return ap.rearrange("p e c -> p c e")

            def over_e(ap):
                return ap.unsqueeze(1).to_broadcast([P, E, NC])

            def first_best(src, best, onehot):
                DV.then(lambda e: e.tensor_reduce(best, by_chunk(src), AX_X, ALU.max))
                DV.then(lambda e: e.tensor_tensor(key, src, over_e(best), ALU.is_equal))
                DV.then(lambda e: e.tensor_tensor(by_chunk(key), by_chunk(key),
                                                  revidx[:, :].unsqueeze(1).to_broadcast([P, NC, E]), ALU.mult), m_rev)
                DV.then(lambda e: e.tensor_reduce(km, by_chunk(key), AX_X, ALU.max))
                DV.then(lambda e: e.tensor_tensor(onehot, key, over_e(km), ALU.is_equal))

            first_best(aff, m1, one)
            DV.then(lambda e: e.tensor_tensor(comb, one, over_e(m1), ALU.mult))
            DV.then(lambda e: e.scalar_tensor_tensor(out=aff, in0=one, scalar=-4.0, in1=aff, op0=ALU.mult, op1=ALU.add))
            first_best(aff, m2, one)
            DV.then(lambda e: e.tensor_tensor(c2, one, over_e(m2), ALU.mult))
            DV.then(lambda e: e.tensor_tensor(comb, comb, c2, ALU.add))
            DV.then(lambda e: e.tensor_tensor(den, m1, m2, ALU.add))
            DV.then(lambda e: e.reciprocal(den, den))
            m = DV.then(lambda e: e.tensor_tensor(comb, comb, over_e(den), ALU.mult))
            bank, free, users = work.take()
            m = PE.do(lambda e: e.transpose(bank[:, 0:P], comb.rearrange("p e c -> p (e c)"), ident[:, :]), m, free)
            m = DV.do(lambda e: e.tensor_copy(c2.rearrange("p e c -> p (e c)"), bank[:, 0:P]), m)
            users.append(m)
            m_scr = SP.copy(stream("scratch"), scratch_e[n].rearrange("e (c t) -> (e c) t", c=NC),
                            c2.rearrange("p e c -> p (e c)"), m)
            m = DV.do(lambda e: e.memset(combT[0:EXPERTS, :], 1.0))
            m_cT = SP.copy(stream("combT"), combT[0:E, :], scratch_e[n], m, m_scr)
            m_res = PO.do(lambda e: e.tensor_tensor(x[:, :, :], x[:, :, :], v[:, :, :], ALU.add), m_v)

            banks = [psum[:, i * BANK:(i + 1) * BANK] for i in range(8)]
            out_free = flat([work.users[i] for i in range(4)])
            up = Ring([(psum[:, 0:BANK], psum[:, BANK:2 * BANK]), (psum[:, 2 * BANK:3 * BANK], psum[:, 3 * BANK:4 * BANK])])
            up.users = [list(wide.users[0]), list(wide.users[1])]
            hidden, rowsof = {}, {}

            def up_half(i, half):
                (wg, wu, wd), m_w, _ = wq[i]
                (bg, bu), free, users = up.take()
                for bank, w in ((bg, wg), (bu, wu)):
                    for k in range(KD):
                        m = PE.do(lambda e, k=k, bank=bank, w=w: e.matmul(
                            bank, w[:, k, :], vT[:, k, half * BANK:(half + 1) * BANK], start=(k == 0), stop=(k == KD - 1)),
                            m_w, m_vT, free, mark=(k == KD - 1))
                gate, g_free, g_users = gate_ring.take()
                hid, h_free, h_users = hid_ring.take()
                m_g = AC.do(lambda e: e.activation(gate, bg, ACT.Gelu, bias=gb[:, i:i + 1]), m, m_gb, g_free)
                if i < E:
                    rb, m_rb, rb_users = rowsof[i]
                    m_g = PO.do(lambda e: e.tensor_tensor(gate, gate, rb[:, half * BANK:(half + 1) * BANK], ALU.mult),
                                m_g, m_rb)
                    rb_users.append(m_g)
                m = DV.do(lambda e: e.scalar_tensor_tensor(out=hid, in0=bu, scalar=ub[:, i:i + 1], in1=gate,
                                                           op0=ALU.add, op1=ALU.mult), m, m_g, m_ub, h_free)
                users += [m, m_g]
                g_users.append(m)
                hidden[i, half] = (hid, m, h_users)

            def out_cols(c):
                return psum[:, 4 * BANK + c * D:4 * BANK + (c + 1) * D]

            def down_half(i, half):
                (wg, wu, wd), m_w, w_users = wq[i]
                hid, m_h, h_users = hidden.pop((i, half))
                for c in range(4 * half, 4 * half + 4):
                    m = PE.do(lambda e, c=c: e.matmul(out_cols(c), hid[:, (c % 4) * P:(c % 4 + 1) * P], wd,
                                                      start=False, stop=(i == order[-1]), skip_group_check=True),
                              m_h, mark=(c % 4 == 3))
                h_users.append(m)
                if half == 1:
                    w_users.append(m)
                return m

            steps = [(i, half) for i in order for half in range(2)]
            for s, (i, half) in enumerate(steps):
                if half == 0:
                    p = order.index(i)
                    for nxt in order[p:p + 3]:
                        if nxt < E and nxt not in rowsof:
                            rowsof[nxt] = load_rows(scratch_e[n][nxt:nxt + 1, :], m_scr)
                up_half(i, half)
                if s == 2:
                    for c in range(NC):
                        PE.do(lambda e, c=c: e.matmul(out_cols(c), combT[0:EXPERTS, c * P:(c + 1) * P],
                                                      b2w[0:EXPERTS, :], start=(c % 2 == 0), stop=False,
                                                      skip_group_check=True), m_cT, m_b2, out_free)
                if s >= 2:
                    down_half(*steps[s - 2])
                if half == 1 and s // 2 + 3 < len(order):
                    load_expert(s // 2 + 3)
            m_last = [down_half(*s) for s in steps[-2:]]
            m_out = []
            for q in range(4):
                m = DV.do(lambda e, q=q: e.tensor_tensor(
                    x[:, 2 * q:2 * q + 2, :], banks[4 + q].rearrange("p (c d) -> p c d", c=2),
                    x[:, 2 * q:2 * q + 2, :], ALU.add), m_last[q // 2], m_res)
                m_out += [m, m]
            join()
            return m_out


        m_x1 = experts(0, m_xa)

        B = Arena()
        w_ring = Ring([B(KD * P).rearrange("p (k m) -> p k m", k=KD) for _ in range(3)])
        cw = B(6 * TAPS).rearrange("p (i k) -> p i k", k=TAPS)
        cb, nw = B(6), B(XT)
        wdt = B(KD * HB).rearrange("p (k h) -> p k h", k=KD)
        dtb, alog, dskip = B(HB), B(HB), B(HB)
        xt = B(XT * T).rearrange("p (i t) -> p i t", i=XT)
        zc = B(XT * T).rearrange("p (i t) -> p i t", i=XT)
        u_padded = B(NC * 4 * SUBS * QUAD).rearrange("p (c j s w) -> p c j s w", c=NC, j=4, s=SUBS)
        early = u_padded.rearrange("p c j s w -> p (c j s w)")
        Bt, Ct, Bs = (early[:, i * T:(i + 1) * T] for i in range(3))
        ud_ring = Ring([early[:, 3 * T + i * WB:3 * T + (i + 1) * WB] for i in range(2)])
        G, intra = B(T), B(T)
        U = B(NC * WB).rearrange("p (c m) -> p c m", c=NC)
        Dx = B(NC * WB).rearrange("p (c m) -> p c m", c=NC)
        y = B(NC * WB).rearrange("p (c m) -> p c m", c=NC)
        st_ring = Ring([B(WB) for _ in range(2)])
        wout = B(XT * D).rearrange("p (i d) -> p i d", i=XT)
        ssq, rms = B(NC), B(NC)
        raw_b = y.rearrange("p c m -> p (c m)")[:, 0:HB * NC]

        m_cw = SP.copy(stream("cw"), cw, io["conv_b"])
        m_cb = SP.copy(stream("cb"), cb, io["convbias_b"])
        m_nw = SP.copy(stream("nw"), nw, io["norm_b"])
        m_wdt = SP.copy(stream("wdt"), wdt, io["wdt_b"])
        m_dtb = SP.copy(stream("dtb"), dtb, io["dtb_b"].to_broadcast([P, HB]))
        m_alog = SP.copy(stream("alog"), alog, io["alog_b"].to_broadcast([P, HB]))
        m_dsk = SP.copy(stream("dskip"), dskip, io["d_b"].to_broadcast([P, HB]))
        m_wout = SP.copy(stream("wo"), wout, io["wout_b"])
        m_cw = DV.do(lambda e: e.tensor_scalar(cw, cw, 0.5, None, ALU.mult), m_cw)
        _, m_vT = layer_norm(m_x1, None)

        def project_b(i):
            w, before, users = w_ring.take()
            m_w = SP.copy(stream(f"wb{i % 3}"), w, io["w_b"][i], before)
            bank, m, b_users = project(lambda k: w[:, k, :], m_w, m_vT)
            users.append(m)
            return bank, m, b_users

        m = project_dt(wdt, m_wdt, HB, dtb, m_dtb, raw_b)
        fb, m_fb, m_scr = decays(HB, raw_b, m, alog, m_alog, scratch_b)
        m_cv = []
        for i, dst in enumerate([Bt, Ct] + [xt[:, q, :] for q in range(XT)]):
            bank, m, users = project_b(i)
            for _ in conv(dst, bank, m, cw[:, i, :], [m_cw, m_cb], None, users, m_cv, bias=cb[:, i:i + 1]):
                pass
        m_z = []
        for q in range(XT):
            bank, m, users = project_b(6 + q)
            m = AC.do(lambda e, q=q, bank=bank: e.activation(zc[:, q, :], bank, ACT.Silu, scale=0.25), m)
            users.append(m)
            m_z.append(m)

        m_bs, m_g, m_u = [], [], []
        for q in range(2):
            bank, free, users = work.take()
            for c in range(4 * q, 4 * q + 4):
                m = PE.do(lambda e, c=c, bank=bank: e.transpose(bank[:, (c % 4) * P:(c % 4 + 1) * P],
                                                                Bt[:, c * P:(c + 1) * P], ident[:, :]), m_cv[0], free)
            m = AC.do(lambda e, q=q, bank=bank: e.copy(Bs[:, q * BANK:(q + 1) * BANK], bank), m)
            users.append(m)
            m_bs.append(m)
            bank, free, users = work.take()
            for c in range(4 * q, 4 * q + 4):
                m = PE.do(lambda e, c=c, bank=bank: e.matmul(bank[:, (c % 4) * P:(c % 4 + 1) * P],
                                                             Bt[:, c * P:(c + 1) * P], Ct[:, c * P:(c + 1) * P],
                                                             start=True, stop=True), m_cv[0:2], free)
            m = AC.do(lambda e, q=q, bank=bank: e.copy(G[:, q * BANK:(q + 1) * BANK], bank), m)
            users.append(m)
            m_g.append(m)

        g3 = G.rearrange("p (c t) -> p c t", t=P)
        m_g = PO.do(lambda e: e.affine_select(out=g3, in_=g3, compare_op=ALU.is_ge, fill=0.0, base=0,
                                              pattern=[[0, NC], [1, P]], channel_multiplier=-1), m_g)

        def per_head(name, c):
            return spread(fb[name].rearrange("p (h c) -> p h c", c=NC)[:, :, c], PB)

        def heads(ap):
            return ap.rearrange("p (h m) -> p h m", m=PB)

        for c in range(NC):
            bank, free, users = work.take()
            for i in range(XT):
                m = PE.do(lambda e, i=i, c=c, bank=bank: e.transpose(bank[:, i * P:(i + 1) * P],
                                                                     xt[:, i, c * P:(c + 1) * P], ident[:, :]),
                          m_cv[2 + i], free)
            m_t = m
            m = DV.do(lambda e, c=c, bank=bank: e.tensor_tensor(heads(U[:, c, :]), heads(bank), per_head("dtl", c),
                                                                ALU.mult), m_t, m_fb)
            m_u.append(m)
            m = DV.do(lambda e, c=c, bank=bank: e.tensor_tensor(heads(Dx[:, c, :]), heads(bank),
                                                                spread(dskip, PB), ALU.mult), m_t, m_dsk)
            users.append(m)

        m_y = []
        m_y.append(PO.do(lambda e: e.memset(y[:, 0, :], 0.0), m_fb))
        st_prev, m_st = None, None
        for c in range(NC - 1):
            (ud, ud_free, ud_users), (st, st_free, st_users) = ud_ring.take(), st_ring.take()
            m = PO.do(lambda e, c=c, ud=ud: e.tensor_tensor(heads(ud), heads(U[:, c, :]), per_head("wd", c), ALU.mult),
                      m_u[c], m_fb, ud_free)
            bank, free, users = work.take()
            m = PE.do(lambda e, c=c, ud=ud, bank=bank: e.matmul(bank, Bs[:, c * P:(c + 1) * P], ud,
                                                                start=True, stop=True), m, m_bs, free)
            ud_users.append(m)
            if c == 0:
                m_st = DV.do(lambda e, st=st, bank=bank: e.tensor_copy(st, bank), m, st_free)
            else:
                md = DV.do(lambda e, c=c, st=st, old=st_prev: e.tensor_tensor(heads(st), heads(old), per_head("dec", c),
                                                                             ALU.mult), m_st, st_free, m_fb)
                m_st = DV.do(lambda e, st=st, bank=bank: e.tensor_tensor(st, bank, st, ALU.add), m, md)
                st_prev_users.append(m_st)
            users.append(m_st)
            st_prev, st_prev_users = st, st_users
            bank, free, users = work.take()
            m = PE.do(lambda e, c=c, st=st, bank=bank: e.matmul(bank, Ct[:, (c + 1) * P:(c + 2) * P], st,
                                                                start=True, stop=True), m_st, m_cv[1], free)
            st_users.append(m)
            m = DV.do(lambda e, c=c, bank=bank: e.tensor_tensor(heads(y[:, c + 1, :]), heads(bank),
                                                                per_head("ehi", c + 1), ALU.mult), m, m_fb)
            users.append(m)
            m_y.append(m)

        spare = [xt[:, i, :] for i in range(XT)] + [vT[:, k, :] for k in range(KD)]
        spare += [v[:, i * 4:(i + 1) * 4, :].rearrange("p c d -> p (c d)") for i in range(2)]
        for buf in spare:
            bcast.append(buf)
            bcast_ring.buffers.append(len(bcast) - 1)
            bcast_ring.users.append([m_u, PE.last()])
        rows = {}
        AHEAD = len(bcast) - 4
        ON_POOL, OF = 8, 16
        by_turn = [16 * i + SUBS * j + s for i in range(XT) for s in range(SUBS) for j in range(4)]

        def load_head(h):
            rows[h] = load_rows(scratch_b[h:h + 1, :], m_scr)

        def exponents(h):
            buf, m, users = rows[h]
            cum = fb["cumhi"][:, h * NC:(h + 1) * NC]
            r3 = buf.rearrange("p (c t) -> p c t", t=P)
            if h * ON_POOL % OF < ON_POOL:
                m = PO.do(lambda e: e.tensor_tensor(r3, r3, spread(cum, P), ALU.subtract), m, m_fb)
                m = PO.do(lambda e: e.affine_select(out=r3, in_=r3, compare_op=ALU.is_ge, fill=MASKED, base=0,
                                                    pattern=[[0, NC], [1, P]], channel_multiplier=-1), m)
            else:
                for c in range(NC):
                    m = DV.do(lambda e: e.tensor_scalar(r3[:, c, :], r3[:, c, :], cum[:, c:c + 1], 0.0,
                                                        ALU.subtract, ALU.min), m, m_fb, mark=(c == NC - 1))
            rows[h] = (buf, m, users)

        def decay_head(h):
            buf, m, users = rows[h]
            rows[h] = (buf, AC.do(lambda e: e.activation(buf, buf, ACT.Exp), m), users)

        m_pad = PO.do(lambda e: e.memset(early, 0.0), m_y, PE.last(), DV.last())
        for n in range(AHEAD):
            load_head(by_turn[n])
        for n in range(3):
            exponents(by_turn[n])
        for n in range(2):
            decay_head(by_turn[n])
        m_yb = []
        pad_users, intra_users = [], []

        def pad(i):
            cs = slice(i * P, (i + 1) * P)
            src = U[:, :, cs].rearrange("p c (j s m) -> p c j s m", j=4, m=PB)
            for s in range(SUBS):
                m = AC.do(lambda e: e.copy(u_padded[:, :, :, s, s * PB:(s + 1) * PB], src[:, :, :, s, :]),
                          m_pad, m_u, pad_users)
            return m

        def finish_tile(i, pair, m, users):
            m = AC.do(lambda e: e.copy(intra, pair), m, intra_users)
            users.append(m)
            ws = slice(i * P, (i + 1) * P)
            for q in range(2):
                cs = slice(4 * q, 4 * q + 4)
                m_t = unit(transposes(lambda c: chunk(intra, 4 * q + c)), 4, [m, m_ident],
                           lambda bank, m: DV.do(lambda e: e.tensor_tensor(
                               y[:, cs, ws], bank.rearrange("p (c m) -> p c m", c=4), y[:, cs, ws], ALU.add), m, m_y))
            intra_users[:] = [PE.last()]
            for q in range(NC // 4):
                cs = slice(4 * q, 4 * q + 4)
                for c in range(4 * q, 4 * q + 4):
                    elo = fb["elo"].rearrange("p (h c) -> p h c", c=NC)[:, 16 * i:16 * (i + 1), c]
                    m = PO.do(lambda e: e.tensor_tensor(heads(y[:, c, ws]), heads(y[:, c, ws]), spread(elo, PB), ALU.mult), m_t)
                m = PO.do(lambda e: e.tensor_tensor(y[:, cs, ws], y[:, cs, ws], Dx[:, cs, ws], ALU.add), m)
            m_yb.append(m)

        late = None
        for n, h in enumerate(by_turn):
            i, s, j = n // 16, n // 4 % SUBS, n % 4
            if n % 16 == 0:
                m_up = pad(i)
                pair, free, p_users = wide.take()
                batch = []
            if n + AHEAD < HB:
                load_head(by_turn[n + AHEAD])
            if n + 3 < HB:
                exponents(by_turn[n + 3])
            if n + 2 < HB:
                decay_head(by_turn[n + 2])
            buf, m, users = rows.pop(h)
            m = DV.do(lambda e: e.tensor_tensor(buf, buf, G, ALU.mult), m, m_g)
            batch.append((buf, m, users))
            if j == 3:
                for c in range(NC):
                    for jj, (buf, m, _) in enumerate(batch):
                        m = PE.do(lambda e: e.matmul(pair[jj * QUAD:(jj + 1) * QUAD, c * P:(c + 1) * P],
                                                     u_padded[:, c, jj, s, :], chunk(buf, c), start=(s == 0 and c % 4 == 0),
                                                     stop=(s == SUBS - 1), skip_group_check=True),
                                  m, m_up, free, mark=(c == NC - 1 and jj == 3))
                for _, _, users in batch:
                    users.append(m)
                batch = []
            if n % 16 == 6 and late is not None:
                finish_tile(*late)
                late = None
            if n % 16 == 15:
                pad_users[:] = [m]
                late = (i, pair, m, p_users)
        finish_tile(*late)
        del bcast[4:]
        m_rows_free = [bcast_ring.users[i] for i in range(len(bcast_ring.buffers))]
        del bcast_ring.buffers[4:], bcast_ring.users[4:]
        m_sq = []
        for c in range(NC):
            m = AC.do(lambda e, c=c: e.activation(U[:, c, :], y[:, c, :], ACT.Square, accum_out=ssq[:, c:c + 1]),
                      m_yb, PE.last())
        m = PO.do(lambda e: e.tensor_scalar(rms, ssq, 1.0 / WB, None, ALU.mult), m)
        m = PO.do(lambda e: e.tensor_scalar(rms, rms, 1e-5, None, ALU.add), m)
        m_rms = PO.do(lambda e: e.tensor_tensor(rms, rms, neghalf[:, 0:NC], ALU.pow), m)
        m_gt = []
        m_x2 = []
        for q in range(2):
            for i in range(XT):
                bank, free, users = work.take()
                for c in range(4 * q, 4 * q + 4):
                    m = PE.do(lambda e, c=c, i=i, bank=bank: e.transpose(bank[:, (c % 4) * P:(c % 4 + 1) * P],
                                                                         y[:, c, i * P:(i + 1) * P], ident[:, :]),
                              m_yb, free)
                ts = slice(q * BANK, (q + 1) * BANK)
                m = DV.do(lambda e, i=i, ts=ts, bank=bank: e.scalar_tensor_tensor(
                    out=xt[:, i, ts], in0=bank, scalar=nw[:, i:i + 1], in1=zc[:, i, ts], op0=ALU.mult, op1=ALU.mult),
                    m, m_z, m_nw, m_rows_free)
                users.append(m)
                m_gt.append(m)
            for c2 in (4 * q, 4 * q + 2):
                bank, free, users = work.take()
                for c in (c2, c2 + 1):
                    for i in range(XT):
                        m = PE.do(lambda e, c=c, i=i, bank=bank: e.matmul(
                            bank[:, (c % 2) * D:(c % 2 + 1) * D], xt[:, i, c * P:(c + 1) * P], wout[:, i, :],
                            start=(i == 0), stop=(i == XT - 1)), m_gt, m_wout, free)
                for c in (c2, c2 + 1):
                    m_c = DV.do(lambda e, c=c, bank=bank: e.scalar_tensor_tensor(
                        out=x[:, c, :], in0=bank[:, (c % 2) * D:(c % 2 + 1) * D], scalar=rms[:, c:c + 1],
                        in1=x[:, c, :], op0=ALU.mult, op1=ALU.add), m, m_rms)
                    m_x2.append(m_c)
                users.append(m_c)
        join()

        m_x3 = experts(1, m_x2)
        m_out = [SP.copy(stream(f"x{c}"), io["out"][c * P:(c + 1) * P, :], x[:, c, :], m_x3[c]) for c in range(NC)]
        SP.wait(m_out)


def kernel(**inputs):
    import concourse.bacc as bacc
    from concourse.bass_utils import run_bass_kernel_spmd

    a = {n: np.ascontiguousarray(np.asarray(t)) for n, t in inputs.items()}

    def k_major(w):
        return w.reshape(KD, P, -1).transpose(1, 0, 2)

    win = a["L0_attn_a_Win"]
    wx, wz = win[:HA * PA], win[HA * PA:2 * HA * PA]
    wb, wc = (win[2 * HA * PA + i * HA * NS:2 * HA * PA + (i + 1) * HA * NS].reshape(PAIRS, 2, NS, D) for i in range(2))
    w_a = np.stack([wx.reshape(PAIRS, P, D), wb[:, 0], wb[:, 1], wc[:, 0], wc[:, 1], wz.reshape(PAIRS, P, D)], 1)
    w_a = w_a.reshape(PAIRS, 6, P, KD, P).transpose(0, 4, 3, 1, 2)
    cb_, cc_ = (a[f"L0_attn_a_conv_w_{n}"].reshape(PAIRS, 2, NS, TAPS) for n in "bc")
    cx_ = a["L0_attn_a_conv_w_x"].reshape(PAIRS, P, TAPS)
    conv_a = np.stack([cx_, cb_[:, 0], cb_[:, 1], cc_[:, 0], cc_[:, 1]], 1).transpose(2, 0, 1, 3)
    wib = a["L0_attn_b_in_proj_w"]
    order = [wib[:, 2 * WB:2 * WB + NS], wib[:, 2 * WB + NS:2 * WB + 2 * NS]]
    order += [wib[:, WB + i * P:WB + (i + 1) * P] for i in range(XT)] + [wib[:, i * P:(i + 1) * P] for i in range(XT)]
    cwb, cbb = a["L0_attn_b_conv_w"], a["L0_attn_b_conv_b"]
    tiles_b = [slice(WB, WB + NS), slice(WB + NS, WB + 2 * NS)] + [slice(i * P, (i + 1) * P) for i in range(XT)]
    f = {n: a[f"L0_ffn_{n}"] for n in ("wa", "rg", "rgb", "rw1", "rb1", "rw2", "rb2", "sg", "sgb", "sw1", "sb1",
                                       "sw2", "sb2")}

    def up(routed, shared):
        return np.concatenate([routed, shared]).reshape(EXPERTS, KD, P, F).transpose(0, 2, 1, 3)

    arrays = {
        "x": a["L0_attn_a_x"].reshape(T, D),
        "w_a": w_a,
        "wdt_a": k_major(win[-HA:].T),
        "conv_a": conv_a,
        "dtb_a": a["L0_attn_a_dt_bias"].reshape(1, HA),
        "alog_a": a["L0_attn_a_A_log"].reshape(1, HA),
        "wout_a": a["L0_attn_a_Wout"].T.reshape(PAIRS // GROUP, GROUP, P, D).transpose(0, 2, 1, 3),
        "w_b": np.stack([k_major(w) for w in order]),
        "wdt_b": k_major(wib[:, -HB:]),
        "conv_b": np.stack([cwb[s] for s in tiles_b], 1),
        "convbias_b": np.stack([cbb[s] for s in tiles_b], 1),
        "norm_b": a["L0_attn_b_norm_w"].reshape(XT, P).T,
        "dtb_b": a["L0_attn_b_dt_bias"].reshape(1, HB),
        "alog_b": a["L0_attn_b_A_log"].reshape(1, HB),
        "d_b": a["L0_attn_b_D"].reshape(1, HB),
        "wout_b": a["L0_attn_b_out_proj_w"].reshape(XT, P, D).transpose(1, 0, 2),
        "wa_e": k_major(f["wa"]),
        "wg": up(f["rg"], f["sg"]),
        "wu": up(f["rw1"], f["sw1"]),
        "wd": np.concatenate([f["rw2"], f["sw2"]]),
        "gb": np.concatenate([f["rgb"], f["sgb"]]).T,
        "ub": np.concatenate([f["rb1"], f["sb1"]]).T,
        "b2": np.concatenate([f["rb2"], f["sb2"]]),
        "ident": np.eye(P, dtype=np.float32),
        "tri": np.triu(np.ones((P, P), np.float32)),
        "revidx": (E - np.arange(E, dtype=np.float32)).reshape(1, E),
    }
    arrays = {n: np.ascontiguousarray(t) for n, t in arrays.items()}
    nc = bacc.Bacc("TRN2", target_bir_lowering=False, num_devices=1)
    io = {n: nc.dram_tensor(f"in_{n}", t.shape, F32, kind="ExternalInput").ap() for n, t in arrays.items()}
    io["out"] = nc.dram_tensor("out", (T, D), F32, kind="ExternalOutput").ap()
    hybrid_block(nc, io)
    r = run_bass_kernel_spmd(nc, [{f"in_{n}": t for n, t in arrays.items()}], core_ids=[0])
    return r.results[0]["out"].reshape(1, T, D)
```

```python
from contextlib import ExitStack

import numpy as np

import concourse.bass as bass
from concourse import mybir
from concourse.alu_op_type import AluOpType as ALU

ACT = mybir.ActivationFunctionType
F32 = mybir.dt.float32
F32R = mybir.dt.float32r
AX_X = mybir.AxisListType.X

P = 128
T, D = 1024, 256
NC = T // P
KD = D // P
TAPS = 4
NS = 128
BANK = 512

HA, PA = 32, 64
PAIRS = HA * PA // P
GROUP = 2
HB, PB = 64, 8
WB = HB * PB
XT = WB // P
QUAD = 32
SUBS = QUAD // PB

E, F, SH = 16, 128, 2
EXPERTS = E + SH
SPLITS = 5

ARENA = 33920
DECAY_FLOOR = -105.0
QUANTUM = 1.5 * 2.0 ** 13
MASKED = -30000.0


class Mark:

    def __init__(self, sem, value):
        self.sem, self.value = sem, value


class Lane:

    def __init__(self, engine, sem):
        self.engine, self.sem, self.count, self.reached = engine, sem, 0, {}

    def wait(self, *marks):
        for m in flat(marks):
            if m.value > self.reached.get(m.sem.name, 0):
                self.engine.wait_ge(m.sem, m.value)
                self.reached[m.sem.name] = m.value

    def do(self, build, *after, mark=True):
        self.wait(*after)
        instruction = build(self.engine)
        if mark:
            instruction.then_inc(self.sem, 1)
            self.count += 1
        return self.last()

    def last(self):
        return Mark(self.sem, self.count)

    def then(self, build, *after):
        return self.do(build, self.last(), *after)

    def copy(self, stream, dst, src, *after):
        self.wait(*after)
        self.engine.dma_start(dst, src).then_inc(stream.sem, 16)
        stream.count += 16
        return Mark(stream.sem, stream.count)


def flat(marks):
    out = []
    for m in marks:
        out += flat(m) if isinstance(m, (list, tuple)) else [m]
    return [m for m in out if m is not None]


class Stream:

    def __init__(self, sem):
        self.sem, self.count = sem, 0


class Ring:

    def __init__(self, buffers):
        self.buffers, self.users, self.n = buffers, [[] for _ in buffers], 0

    def take(self):
        i = self.n % len(self.buffers)
        self.n += 1
        before, self.users[i] = self.users[i], []
        return self.buffers[i], before, self.users[i]

    def grow(self, buffers, marks):
        assert self.n % len(self.buffers) == 0, "in the middle of a turn"
        self.n = len(self.buffers)
        self.buffers += buffers
        self.users += [[marks] for _ in buffers]


def spread(ap, n):
    return ap.unsqueeze(len(ap.shape)).to_broadcast([*ap.shape, n])


def hybrid_block(nc, io):
    with ExitStack() as ctx:
        def sb(name, shape, dtype=F32):
            return ctx.enter_context(nc.sbuf_tensor(name, shape, dtype))

        def sem(name):
            return ctx.enter_context(nc.semaphore(name))

        PE, AC, DV, PO, SP = (Lane(engine, sem(f"{name}_done")) for name, engine in (
            ("pe", nc.tensor), ("act", nc.scalar), ("dve", nc.vector), ("pool", nc.gpsimd), ("sp", nc.sync)))

        x = sb("x", [P, NC, D])
        v = sb("v", [P, NC, D])
        vT = sb("vT", [P, 2, KD, T], F32R)
        ident = sb("ident", [P, P])
        tri = sb("tri", [P, P])
        ones = sb("ones", [P, P])
        revidx = sb("revidx", [P, E])
        neghalf = sb("neghalf", [P, 2 * NC])
        bn6 = sb("bn6", [P, NC, 6])
        bn2 = sb("bn2", [P, NC, 2])
        rstd = sb("rstd", [P, NC])
        eps_rstd = sb("eps_rstd", [P, NC])
        bcast = [sb(f"bcast{i}", [P, T])[:, :] for i in range(4)]
        split = sb("split", [P, SPLITS, 2, KD, P], F32R)
        split_down = sb("split_down", [P, 3, 2, D], F32R)
        split_hid = sb("split_hid", [P, 2, 2, BANK], F32R)
        narrow = sb("narrow", [P, 2, KD, HB], F32R)
        arena = sb("arena", [P, ARENA])
        psum = ctx.enter_context(nc.psum_tensor("psum", [P, 8 * BANK], F32))
        wide = Ring([psum[:, 2 * i * BANK:(2 * i + 2) * BANK] for i in range(2)])
        work = Ring([psum[:, i * BANK:(i + 1) * BANK] for i in range(4, 8)])

        scratch_a = nc.dram_tensor("scratch_a", [HA, T], F32).ap()
        scratch_b = nc.dram_tensor("scratch_b", [HB, T], F32).ap()
        scratch_e = [nc.dram_tensor(f"scratch_e{i}", [E, T], F32).ap() for i in range(2)]

        streams = {}

        def stream(name):
            if name not in streams:
                streams[name] = Stream(sem(f"dma_{name}"))
            return streams[name]

        bcast_ring = Ring(list(enumerate(bcast)))

        def load_rows(ring, row, *after):
            (i, buf), before, users = ring.take()
            return buf, SP.copy(stream(f"bcast{i}"), buf, row.to_broadcast([P, T]), before, *after), users

        def queued():
            return [L.last() for L in (PE, AC, DV, PO)] + [Mark(s.sem, s.count) for s in streams.values()]

        def join(marks):
            for L in (PE, AC, DV, PO, SP):
                L.wait(marks)

        m_x = [SP.copy(stream(f"x{c}"), x[:, c, :], io["x"][c * P:(c + 1) * P, :]) for c in range(NC)]
        m_ident = SP.copy(stream("ident"), ident[:, :], io["ident"])
        m_tri = SP.copy(stream("tri"), tri[:, :], io["tri"])
        m_rev = SP.copy(stream("rev"), revidx[:, :], io["revidx"].to_broadcast([P, E]))
        m_ones = PO.do(lambda e: e.memset(ones[:, :], 1.0))
        m_half = PO.do(lambda e: e.memset(neghalf[:, :], -0.5))

        def layer_norm(m_in, before, aside=None):
            done, m_rstd, LATE = [], [], 3
            split_chunks = []

            def rest():
                for src, hi, lo, m_hi, users in split_chunks:
                    m = DV.do(lambda e: e.tensor_tensor(lo, src, hi.bitcast(F32), ALU.subtract), m_hi, before)
                    users.append(m)
                    done.append(m)
                split_chunks.clear()

            for late in range(NC + LATE):
                if late < NC:
                    c = late
                    m = DV.do(lambda e: e.bn_stats(bn6[:, c, :], x[:, c, :]), m_in[c], before)
                    m = DV.do(lambda e: e.bn_aggr(bn2[:, c, :], bn6[:, c, :]), m)
                    m = PO.do(lambda e: e.tensor_scalar(eps_rstd[:, c:c + 1], bn2[:, c, 1:2], 1e-5, None, ALU.add), m)
                    m_rstd.append(PO.do(lambda e: e.tensor_tensor(rstd[:, c:c + 1], eps_rstd[:, c:c + 1],
                                                                  neghalf[:, 0:1], ALU.pow), m, m_half))
                if late == NC and aside is not None:
                    aside()
                c = late - LATE
                if c < 0:
                    continue
                m_v = DV.do(lambda e: e.tensor_scalar(v[:, c, :], x[:, c, :], bn2[:, c, 0:1], rstd[:, c:c + 1],
                                                      ALU.subtract, ALU.mult), m_rstd[c], before)
                if c % 2 == 0:
                    bank, free, users = work.take()
                for k in range(KD):
                    o = bank[:, ((c % 2) * KD + k) * P:((c % 2) * KD + k + 1) * P]
                    m = PE.do(lambda e: e.transpose(o, v[:, c, k * P:(k + 1) * P], ident[:, :]), m_v, m_ident, free)
                if c % 2 == 0:
                    rest()
                else:
                    src = bank.rearrange("p (c k t) -> p k c t", c=2, k=KD)
                    hi, lo = (vT[:, i, :, (c - 1) * P:(c + 1) * P].rearrange("p k (c t) -> p k c t", c=2)
                              for i in range(2))
                    split_chunks.append((src, hi, lo, AC.do(lambda e: e.copy(hi, src), m, before), users))
            rest()
            return [m_v], done

        def softplus(raw, n, dst, tmp, m):
            pos, e_, u, l = (tmp[i][:, 0:n] for i in range(4))
            DV.then(lambda e: e.tensor_scalar(pos, raw, 0.0, None, ALU.max), m)
            m = DV.then(lambda e: e.scalar_tensor_tensor(out=e_, in0=pos, scalar=-2.0, in1=raw, op0=ALU.mult, op1=ALU.add))
            m = AC.do(lambda e: e.activation(e_, e_, ACT.Exp), m)
            yield
            m = DV.do(lambda e: e.tensor_scalar(u, e_, 1.0, None, ALU.add), m)
            m_l = AC.do(lambda e: e.activation(l, u, ACT.Ln), m)
            yield
            DV.then(lambda e: e.scalar_tensor_tensor(out=e_, in0=u, scalar=-1.0, in1=e_, op0=ALU.add, op1=ALU.subtract))
            DV.then(lambda e: e.tensor_tensor(pos, pos, l, ALU.add), m_l)
            DV.then(lambda e: e.reciprocal(u, u), m_l)
            DV.then(lambda e: e.tensor_tensor(u, u, e_, ALU.mult))
            DV.then(lambda e: e.tensor_tensor(dst, pos, u, ALU.subtract))
            yield

        def split_narrow(w, m_w, width):
            hi, lo = narrow[:, 0, :, 0:width], narrow[:, 1, :, 0:width]
            m = DV.do(lambda e: e.tensor_copy(hi, w), m_w, PE.last())
            return DV.do(lambda e: e.tensor_tensor(lo, w, hi.bitcast(F32), ALU.subtract), m)

        PRODUCTS = ((0, 0), (1, 0), (0, 1))

        def project_narrow(width, m_w, m_vT):
            (_, buf), rows_free, rows_users = bcast_ring.take()
            rows = buf[0:width, :]
            for half in range(2):
                bank, free, users = work.take()
                for n, (k, (i, j)) in enumerate((k, p) for k in range(KD) for p in PRODUCTS):
                    m = PE.do(lambda e: e.matmul(bank[0:width, :], narrow[:, i, k, 0:width],
                                                 vT[:, j, k, half * BANK:(half + 1) * BANK],
                                                 start=(n == 0), stop=(n == 3 * KD - 1)),
                              of_half(m_vT, half), m_w, free, mark=(n == 3 * KD - 1))
                m = AC.do(lambda e: e.copy(rows[:, half * BANK:(half + 1) * BANK], bank[0:width, :]), m, rows_free)
                users.append(m)
            bank, free, users = work.take()
            for c in range(NC):
                m_t = PE.do(lambda e: e.transpose(bank[:, c * width:(c + 1) * width], rows[:, c * P:(c + 1) * P],
                                                  ident[0:width, 0:width]), m, m_ident, free)
            rows_users.append(m_t)
            return bank, m_t, users

        def of_half(m_vT, half):
            return m_vT[half * NC // 4:(half + 1) * NC // 4]

        def decays(f, H, raw, m_raw, a_log, m_alog, scratch, small, skip=None, m_skip=None):
            n = H * NC
            for i, name in enumerate(("dt", "t1", "hi", "cumlo", "tothi", "totlo", "t0", "t2", "t3", "lo", "cumhi",
                                      "wd", "dec")):
                f[name] = small[:, i, :]
            yield from softplus(raw, n, f["dt"], [f[t] for t in ("t0", "t1", "t2", "t3")], m_raw)
            a = f["t0"]
            m_ea = AC.do(lambda e: e.activation(a_log, a_log, ACT.Exp), m_alog)
            DV.then(lambda e: e.scalar_tensor_tensor(out=a.rearrange("p (h c) -> p h c", c=NC),
                                                     in0=f["dt"].rearrange("p (h c) -> p h c", c=NC), scalar=-1.0,
                                                     in1=spread(a_log, NC), op0=ALU.mult, op1=ALU.mult), m_ea)
            yield
            DV.then(lambda e: e.tensor_scalar(a, a, DECAY_FLOOR, None, ALU.max))
            DV.then(lambda e: e.tensor_scalar(f["hi"], a, QUANTUM, None, ALU.add))
            DV.then(lambda e: e.tensor_scalar(f["hi"], f["hi"], QUANTUM, None, ALU.subtract))
            m = DV.then(lambda e: e.tensor_tensor(f["lo"], a, f["hi"], ALU.subtract))
            for lhs, m_lhs, src, dst in ((tri, m_tri, "hi", "cumhi"), (tri, m_tri, "lo", "cumlo"),
                                         (ones, m_ones, "hi", "tothi"), (ones, m_ones, "lo", "totlo")):
                bank, free, users = work.take()
                mp = PE.do(lambda e, lhs=lhs, src=src, bank=bank: e.matmul(bank[:, 0:n], lhs[:, :], f[src],
                                                                           start=True, stop=True), m, m_lhs, free)
                m_c = DV.do(lambda e, dst=dst, bank=bank: e.tensor_copy(f[dst], bank[:, 0:n]), mp)
                users.append(m_c)
                yield
                if dst == "cumhi":
                    f["cum_there"] = m_c
                    bank, free, users = work.take()
                    for q in range(n // P):
                        mp = PE.do(lambda e, q=q, bank=bank: e.transpose(
                            bank[:, q * P:(q + 1) * P], f["cumhi"][:, q * P:(q + 1) * P], ident[:, :]), m_c, m_ident, free)
                    rows = f["t1"]
                    m_r = DV.do(lambda e, bank=bank: e.tensor_copy(rows, bank[:, 0:n]), mp)
                    users.append(m_r)
                    f["rows"] = SP.copy(stream("scratch"), scratch.rearrange("(q g) (c t) -> (g c) q t", q=n // P, c=NC),
                                    rows.rearrange("p (q t) -> p q t", t=P), m_r)
                    yield
            AC.do(lambda e: e.activation(f["t2"], f["cumlo"], ACT.Exp), DV.last())
            m = AC.do(lambda e: e.activation(f["t3"], f["cumlo"], ACT.Exp, scale=-1.0))
            yield
            f["elo"], f["ehi"] = f["t2"], f["t0"]
            if skip is not None:
                f["skip"] = f["lo"]
                DV.then(lambda e: e.tensor_tensor(f["skip"].rearrange("p (h c) -> p h c", c=NC),
                                                  f["t3"].rearrange("p (h c) -> p h c", c=NC), spread(skip, NC),
                                                  ALU.mult), m, m_skip)
            m_dtl = DV.then(lambda e: e.tensor_tensor(f["t3"], f["t3"], f["dt"], ALU.mult), m)
            f["dtl"] = f["t3"]
            AC.do(lambda e: e.activation(f["ehi"], f["cumhi"], ACT.Exp))
            yield
            DV.then(lambda e: e.tensor_tensor(f["wd"], f["tothi"], f["cumhi"], ALU.subtract))
            DV.then(lambda e: e.tensor_tensor(f["wd"], f["wd"], f["totlo"], ALU.add))
            m = DV.then(lambda e: e.tensor_tensor(f["dec"], f["tothi"], f["totlo"], ALU.add))
            AC.do(lambda e: e.activation(f["wd"], f["wd"], ACT.Exp), m)
            m = AC.do(lambda e: e.activation(f["dec"], f["dec"], ACT.Exp))
            f["marks"] = [m, m_dtl]
            yield

        def conv(tile_out, bank, m_pe, w, m_w, free, users, marks, bias=None, spare=None):
            for half in range(2):
                hs = slice(half * BANK, (half + 1) * BANK)
                m = AC.do(lambda e: e.activation(tile_out[:, hs], bank[:, hs], ACT.Identity, scale=w[:, TAPS - 1:TAPS],
                                                 bias=0.0 if bias is None else bias), m_pe[half], m_w, free)
            if spare is not None:
                term, term_free, term_users = spare.take()
                far = TAPS - 1
                m = m_term = AC.do(lambda e: e.activation(term[:, far:T], bank[:, 0:T - far], ACT.Identity,
                                                          scale=w[:, 0:1], bias=0.0),
                               m_pe, term_free)
            late_silu()
            for s in range(1, TAPS if spare is None else TAPS - 1):
                yield
                m = DV.do(lambda e, s=s: e.scalar_tensor_tensor(
                    out=tile_out[:, s:T], in0=bank[:, 0:T - s], scalar=w[:, TAPS - 1 - s:TAPS - s],
                    in1=tile_out[:, s:T], op0=ALU.mult, op1=ALU.add), m, m_w)
            users.append(m)
            if spare is not None:
                m = PO.do(lambda e: e.tensor_tensor(tile_out[:, far:T], tile_out[:, far:T], term[:, far:T], ALU.add),
                          m, m_term)
                term_users.append(m)
            yield
            silus.append((tile_out, m, marks))

        silus = []

        def late_silu():
            for tile_out, m, marks in silus:
                marks.append(AC.do(lambda e: e.activation(tile_out, tile_out, ACT.Silu), m))
            silus.clear()

        split_ring = Ring([split[:, i] for i in range(SPLITS)])

        def split_tile(raw, m_raw):
            w, free, users = split_ring.take()
            m = AC.do(lambda e: e.copy(w[:, 0], raw), m_raw, free)
            m = PO.do(lambda e: e.tensor_tensor(w[:, 1], raw, w[:, 0].bitcast(F32), ALU.subtract), m, free)
            return w, m, users

        def product(bank, w, half, m_w, m_vT, free):
            for n, (k, (i, j)) in enumerate((k, p) for k in range(KD) for p in PRODUCTS):
                m = PE.do(lambda e: e.matmul(bank, w[:, i, k, :], vT[:, j, k, half * BANK:(half + 1) * BANK],
                                             start=(n == 0), stop=(n == 3 * KD - 1)),
                          m_w, of_half(m_vT, half), free, mark=(n == 3 * KD - 1))
            return m

        def project(w, m_w, w_users, m_vT):
            bank, free, users = wide.take()
            m = [product(bank[:, half * BANK:(half + 1) * BANK], w, half, m_w, m_vT, free) for half in range(2)]
            w_users.append(m)
            return bank, m, users

        class Arena:

            def __init__(self):
                self.at = 0

            def __call__(self, n):
                self.at += n
                assert self.at <= ARENA, self.at
                return arena[:, self.at - n:self.at]

        A = Arena()
        TILES = 6
        CONV = TILES - 1
        w_ring = Ring([A(KD * TILES * P).rearrange("p (k i m) -> p k i m", k=KD, i=TILES) for _ in range(2)])
        cv_ring = Ring([A(CONV * T).rearrange("p (i t) -> p i t", i=CONV) for _ in range(2)])
        z_ring = Ring([A(T) for _ in range(3)])
        cw = A(PAIRS * 5 * TAPS).rearrange("p (j i k) -> p j i k", i=5, k=TAPS)
        wdt = A(KD * HA).rearrange("p (k h) -> p k h", k=KD)
        dtb, alog = A(HA), A(HA)
        raw_a = A(HA * NC)
        small_a = A(13 * HA * NC).rearrange("p (i n) -> p i n", i=13)
        u_ring = Ring([(A(T).rearrange("p (c m) -> p c m", c=NC), A(T).rearrange("p (c m) -> p c m", c=NC))])
        bt_ring = Ring([A(T) for _ in range(2)])
        st_ring = Ring([A(NC * PA).rearrange("p (c m) -> p c m", c=NC) for _ in range(2)])
        y_ring = Ring([A(T).rearrange("p (c m) -> p c m", c=NC) for _ in range(2)])
        y2 = v[:, 0:NC // 2, :].rearrange("p c d -> p (c d)")
        term_ring = Ring([v[:, NC // 2:NC, :].rearrange("p c d -> p (c d)")])
        LIGHT = (1, 3)
        elo2 = A(HA * NC)
        gated = Ring([A(GROUP * T).rearrange("p (g t) -> p g t", g=GROUP) for _ in range(2)])
        wout_ring = Ring([A(GROUP * D).rearrange("p (g d) -> p g d", g=GROUP) for _ in range(2)])
        nrm = [A(2 * NC) for _ in range(2)]

        m_cw = SP.copy(stream("cw"), cw, io["conv_a"])
        m_wdt = SP.copy(stream("wdt"), wdt, io["wdt_a"])
        m_dtb = SP.copy(stream("dtb"), dtb, io["dtb_a"].to_broadcast([P, HA]))
        m_alog = SP.copy(stream("alog"), alog, io["alog_a"].to_broadcast([P, HA]))
        wq = {}

        def load_pair(j):
            w, before, users = w_ring.take()
            wq[j] = (w, SP.copy(stream(f"wa{j % 2}"), w, io["w_a"][j], before), users)

        load_pair(0)
        load_pair(1)
        m_zero = [PO.do(lambda e, b=b: e.memset(b[:, 0, :], 0.0)) for b in st_ring.buffers]

        split_a = {}

        def split_weights(j, i):
            for n in range(len(split_a), min(j * TILES + i + SPLITS - 1, PAIRS * TILES)):
                jj, ii = n // TILES, n % TILES
                w, m_w, users = wq[jj]
                split_a[n] = split_tile(w[:, :, ii, :], m_w)
                if ii == TILES - 1:
                    users.append(split_a[n][1])
                    if jj + 2 < PAIRS:
                        load_pair(jj + 2)
            return split_a[j * TILES + i]

        _, m_vT = layer_norm(m_x, None, lambda: split_weights(0, 0))

        def project_dt(wdt, m_wdt, H, bias, m_bias, raw):
            m = split_narrow(wdt, m_wdt, H)
            bank, m, users = project_narrow(H, m, m_vT)
            m = DV.do(lambda e: e.tensor_tensor(raw.rearrange("p (h c) -> p h c", c=NC),
                                                bank[:, 0:H * NC].rearrange("p (c h) -> p h c", c=NC),
                                                spread(bias, NC), ALU.add), m, m_bias)
            users.append(m)
            return m

        fa, m_fa = {}, []

        def fac(name, h):
            return fa[name][:, h * NC:(h + 1) * NC]

        conv_out, z_out, rows, heads_y, group = {}, {}, {}, {}, {}

        def project_pair(j):
            out, free, users = cv_ring.take()
            zt, z_free, z_users = z_ring.take()
            marks = []
            conv_out[j] = (out, marks, users)
            for i in range(CONV):
                bank, m, b_users = project(*split_weights(j, i), m_vT)
                yield from conv(out[:, i, :], bank, m, cw[:, j, i, :], m_cw, free, b_users, marks,
                                spare=term_ring if i in LIGHT else None)
                yield
            bank, m, b_users = project(*split_weights(j, CONV), m_vT)
            yield
            m = AC.do(lambda e: e.activation(zt, bank, ACT.Silu), m, z_free)
            b_users.append(m)
            z_out[j] = (zt, m, z_users)
            late_silu()
            yield

        PROJECT_STEPS = 5 * CONV + 2

        def load_decays(j):
            for h in (2 * j, 2 * j + 1):
                rows[h] = load_rows(bcast_ring, scratch_a[h:h + 1, :], fa["rows"])

        def exponents_head(h):
            buf, m, users = rows[h]
            r3 = buf.rearrange("p (c t) -> p c t", t=P)
            m = PO.do(lambda e: e.tensor_tensor(r3, r3, spread(fac("cumhi", h), P), ALU.subtract), m, fa["cum_there"])
            m = PO.do(lambda e: e.affine_select(out=r3, in_=r3, compare_op=ALU.is_ge, fill=MASKED, base=0,
                                                pattern=[[0, NC], [1, P]], channel_multiplier=-1), m)
            rows[h] = (buf, m, users)

        def decay_pair(j):
            for h in (2 * j, 2 * j + 1):
                buf, m, users = rows[h]
                rows[h] = (buf, AC.do(lambda e: e.activation(buf, buf, ACT.Exp), m), users)

        def unit(columns, n, after, evacuate):
            bank, free, users = work.take()
            for i in range(n):
                m = PE.do(columns(bank, i), after, free, mark=(i == n - 1))
            m = evacuate(bank, m)
            users.append(m)
            return m

        def transposes(src):
            return lambda bank, i: lambda e: e.transpose(bank[:, i * P:(i + 1) * P], src(i), ident[:, :])

        def chunk(ap, c):
            return ap[:, c * P:(c + 1) * P]

        def scan_pair(j):
            out, m_cv, cv_users = conv_out.pop(j)
            (U, Ud), u_free, u_users = u_ring.take()
            m_u = []

            def scale_u(q):
                cs = slice(4 * q, 4 * q + 4)

                def both(ap):
                    return ap[:, cs, :].rearrange("p c (g m) -> p c g m", g=2)

                def factor(name):
                    f = fa[name][:, 2 * j * NC:(2 * j + 2) * NC].rearrange("p (g c) -> p c g", g=2)
                    return spread(f[:, cs, :], PA)

                def evacuate(bank, m):
                    return DV.do(lambda e: e.tensor_tensor(both(U), bank.rearrange("p (c g m) -> p c g m", c=4, g=2),
                                                           factor("dtl"), ALU.mult), m, m_fa, u_free)
                m = unit(transposes(lambda i: chunk(out[:, 0, :], 4 * q + i)), 4, [m_cv[0], m_ident], evacuate)
                m_u.append(PO.do(lambda e: e.tensor_tensor(both(Ud), both(U), factor("wd"), ALU.mult), m, m_fa, u_free))

            y, y_free, y_users = y_ring.take()
            head = [{}, {}]

            def turn_b(g, q):
                s = head[g]
                if q == 0:
                    s["bt"], s["bt_free"], s["bt_users"] = bt_ring.take()
                    s["m_bt"] = []
                s["m_bt"].append(unit(
                    transposes(lambda i: chunk(out[:, 1 + g, :], 4 * q + i)), 4, [m_cv[1 + g], m_ident],
                    lambda bank, m: AC.do(lambda e: e.copy(s["bt"][:, q * BANK:(q + 1) * BANK], bank), m, s["bt_free"])))

            def mix(g, q):
                s = head[g]
                buf, m_e, _ = rows[2 * j + g]
                half = buf[:, q * BANK:(q + 1) * BANK]
                s.setdefault("m_m", []).append(unit(
                    lambda bank, i: lambda e: e.matmul(chunk(bank, i), chunk(out[:, 1 + g, :], 4 * q + i),
                                                       chunk(out[:, 3 + g, :], 4 * q + i), start=True, stop=True),
                    4, [m_cv[1 + g], m_cv[3 + g]],
                    lambda bank, m: DV.do(lambda e: e.tensor_tensor(half, bank, half, ALU.mult), m, m_e)))

            def states():
                banks = []
                for g in range(2):
                    s = head[g]
                    bank, free, users = work.take()
                    for c in range(NC - 1):
                        m = PE.do(lambda e: e.matmul(bank[:, c * PA:(c + 1) * PA], chunk(s["bt"], c),
                                                     Ud[:, c, g * PA:(g + 1) * PA], start=True, stop=True),
                                  s["m_bt"], m_u, free, mark=(c == NC - 2))
                    s["bt_users"].append(m)
                    s["st"], st_free, s["st_users"] = st_ring.take()
                    banks.append((bank, users))
                    s["m_st"] = [m, st_free]
                    yield
                for c in range(NC - 1):
                    for g in range(2):
                        s = head[g]
                        st = s["st"]
                        s["m_st"] = [DV.do(lambda e: e.scalar_tensor_tensor(
                            out=st[:, c + 1, :], in0=st[:, c, :], scalar=fac("dec", 2 * j + g)[:, c:c + 1],
                            in1=banks[g][0][:, c * PA:(c + 1) * PA], op0=ALU.mult, op1=ALU.add),
                            s["m_st"], m_fa, m_zero)]
                    if c % 3 == 2:
                        yield
                for g in range(2):
                    banks[g][1].extend(head[g]["m_st"])

            def outputs(g):
                s = head[g]
                hs = slice(g * PA, (g + 1) * PA)
                bank_i, free, users_i = work.take()
                buf, _, e_users = rows.pop(2 * j + g)
                for c in range(NC):
                    m_i = PE.do(lambda e: e.matmul(bank_i[:, c * PA:(c + 1) * PA], chunk(buf, c), U[:, c, hs],
                                                   start=True, stop=True), s["m_m"], m_u, free, mark=(c == NC - 1))
                e_users.append(m_i)
                yield
                m = unit(lambda bank, c: lambda e: e.matmul(bank[:, c * PA:(c + 1) * PA], chunk(out[:, 3 + g, :], c),
                                                            s["st"][:, c, :], start=True, stop=True),
                         NC, [s["m_st"]],
                         lambda bank, m: DV.do(lambda e: e.tensor_tensor(
                             y[:, :, hs], bank.rearrange("p (c m) -> p c m", c=NC), spread(fac("ehi", 2 * j + g), PA),
                             ALU.mult), m, y_free))
                s["st_users"].append(PE.last())
                yield
                m = DV.do(lambda e: e.tensor_tensor(y[:, :, hs], bank_i.rearrange("p (c m) -> p c m", c=NC),
                                                    y[:, :, hs], ALU.add), m, m_i)
                users_i.append(m)
                s["m_y"] = m
                yield

            scale_u(0)
            yield
            scale_u(1)
            yield
            for g in range(2):
                for q in range(2):
                    turn_b(g, q)
                    yield
            yield from project_out(1)
            mix(0, 0)
            yield
            mix(0, 1)
            yield
            norm_pair(j - 1)
            yield from states()
            mix(1, 0)
            yield
            mix(1, 1)
            yield
            yield from outputs(0)
            yield from project_out(1)
            yield from outputs(1)
            yield from finish_pair(j - 1)
            u_users.append(PE.last())
            cv_users.append(PE.last())
            m = AC.do(lambda e: e.activation(y2.rearrange("p (c m) -> p c m", c=NC), y, ACT.Square),
                      head[0]["m_y"], head[1]["m_y"], y2_users)
            heads_y[j] = (y, m, y_users)
            yield

        def norm_pair(j):
            if j < 0:
                return
            y, m, y_users = heads_y[j]
            m = DV.do(lambda e: e.tensor_reduce(nrm[0].rearrange("p (g c) -> p g c", g=2),
                                                y2.rearrange("p (c g m) -> p g c m", c=NC, g=2), AX_X, ALU.add), m,
                      nrm_users)
            y2_users[:] = [m]
            pr = slice(2 * j * NC, (2 * j + 2) * NC)
            m = PO.do(lambda e: e.tensor_tensor(nrm[1], nrm[0], elo2[:, pr], ALU.mult), m)
            nrm_users[:] = [m]
            m = PO.do(lambda e: e.tensor_scalar(nrm[1], nrm[1], 1e-6, None, ALU.add), m)
            m = PO.do(lambda e: e.tensor_tensor(nrm[1], nrm[1], neghalf[:, 0:2 * NC], ALU.pow), m)
            m = PO.do(lambda e: e.tensor_tensor(nrm[1], nrm[1], fa["elo"][:, pr], ALU.mult), m)
            for g in range(2):
                hs = slice(g * PA, (g + 1) * PA)
                m = PO.do(lambda e: e.tensor_tensor(y[:, :, hs], y[:, :, hs],
                                                    spread(nrm[1][:, g * NC:(g + 1) * NC], PA), ALU.mult), m)
            heads_y[j] = (y, m, y_users)

        y2_users, nrm_users = [], []
        m_xa = [None] * (NC // 2)

        def finish_pair(j):
            if j < 0:
                return
            y, m_y, y_users = heads_y.pop(j)
            zt, m_z, z_users = z_out.pop(j)
            if j % GROUP == 0:
                gt, g_free, g_users = gated.take()
                wo, w_free, w_users = wout_ring.take()
                m_wo = SP.copy(stream(f"wo{j // GROUP % 2}"), wo, io["wout_a"][j // GROUP], w_free)
                group.update(gt=gt, free=g_free, users=g_users, wo=wo, m_wo=m_wo, w_users=w_users, m=[])
            gt = group["gt"]
            for q in range(2):
                ts = slice(q * BANK, (q + 1) * BANK)
                m = unit(transposes(lambda i: y[:, 4 * q + i, :]), 4, [m_y, m_ident],
                         lambda bank, m: DV.do(lambda e: e.tensor_tensor(gt[:, j % GROUP, ts], bank, zt[:, ts], ALU.mult),
                                               m, m_z, group["free"]))
                group["m"].append(m)
                yield
            y_users.append(PE.last())
            z_users.append(m)
            if j % GROUP == GROUP - 1:
                full.extend((dict(group), q) for q in range(NC // 2))

        full = []

        def project_out(n):
            for _ in range(min(n, len(full))):
                g_, q = full.pop(0)
                gt, wo = g_["gt"], g_["wo"]

                def products(bank, i):
                    c, g = 2 * q + i // GROUP, i % GROUP
                    return lambda e: e.matmul(bank[:, (c % 2) * D:(c % 2 + 1) * D], gt[:, g, c * P:(c + 1) * P],
                                              wo[:, g, :], start=(g == 0), stop=(g == GROUP - 1))
                xs = x[:, 2 * q:2 * q + 2, :]
                m_xa[q] = unit(products, 2 * GROUP, [g_["m"], g_["m_wo"]],
                               lambda bank, m: DV.do(lambda e: e.tensor_tensor(
                                   xs, bank.rearrange("p (c d) -> p c d", c=2), xs, ALU.add), m, m_xa[q]))
                if q == NC // 2 - 1:
                    g_["users"].append(PE.last())
                    g_["w_users"].append(PE.last())
                yield

        SCAN_STEPS = 25
        DECAY_STEPS = 13
        WAIT_ROWS = 3

        def interleave(first, n_first, second, n_second):
            done = [0, 0]
            live = [first, second]
            while any(live):
                rate = [done[0] / n_first if live[0] else 9e9, done[1] / n_second if live[1] else 9e9]
                i = 0 if rate[0] <= rate[1] else 1
                if next(live[i], live) is live:
                    live[i] = None
                done[i] += 1

        def pair_steps(j):
            if j + 1 < PAIRS:
                load_decays(j + 1)
            for n, _ in enumerate(scan_pair(j)):
                if n in (10, 15) and j + 1 < PAIRS:
                    exponents_head(2 * (j + 1) + (n == 15))
                if n == 18 and j + 1 < PAIRS:
                    decay_pair(j + 1)
                yield

        def first_decays():
            m_raw = project_dt(wdt, m_wdt, HA, dtb, m_dtb, raw_a)
            yield
            n = 0
            for _ in decays(fa, HA, raw_a, m_raw, alog, m_alog, scratch_a, small_a):
                if "rows" in fa:
                    if n == 0:
                        load_decays(0)
                    if n in (WAIT_ROWS, WAIT_ROWS + 1):
                        exponents_head(n - WAIT_ROWS)
                    if n == WAIT_ROWS + 2:
                        decay_pair(0)
                    n += 1
                yield
            assert n > WAIT_ROWS + 2
            DV.then(lambda e: e.tensor_tensor(elo2, fa["elo"], fa["elo"], ALU.mult), fa["marks"])
            m_fa.extend(fa["marks"] + [DV.then(lambda e: e.tensor_scalar(elo2, elo2, 1.0 / PA, None, ALU.mult))])

        pair = project_pair(0)
        next(pair)
        interleave(first_decays(), DECAY_STEPS + 3, pair, PROJECT_STEPS)
        for j in range(PAIRS):
            interleave(pair_steps(j), SCAN_STEPS, project_pair(j + 1) if j + 1 < PAIRS else None, PROJECT_STEPS)
        norm_pair(PAIRS - 1)
        for _ in project_out(len(full)):
            pass
        for _ in finish_pair(PAIRS - 1):
            pass
        for _ in project_out(len(full)):
            pass
        m_xa = [m_xa[c // 2] for c in range(NC)]
        v_free = [y2_users, term_ring.users, PE.last()]
        weights_free = w_ring.users

        def experts(n, m_in, before, weights_free):
            m_phase = queued()
            G = Arena()
            wg_ring = Ring([tuple(G(KD * F).rearrange("p (k f) -> p k f", k=KD) for _ in range(2)) + (G(D),)
                            for _ in range(4)])
            wa = G(KD * E).rearrange("p (k e) -> p k e", k=KD)
            gb, ub = G(EXPERTS), G(EXPERTS)
            aff, key, one, comb, c2 = (G(NC * E).rearrange("p (e c) -> p e c", c=NC) for _ in range(5))
            m1, m2, km, den = (G(NC) for _ in range(4))
            combT = G(T)
            b2w = G(D)
            gate_ring = Ring([G(BANK) for _ in range(3)])
            hid_ring = Ring([G(BANK) for _ in range(2)])
            hid2_ring = Ring([split_hid[:, i] for i in range(2)])
            down_ring = Ring([split_down[:, i] for i in range(3)])
            BIAS_AT = 8
            wq = {}
            order = list(range(E, EXPERTS)) + list(range(E))

            def load_expert(p):
                i = order[p]
                w, before, users = wg_ring.take()
                got = []
                for part, name in zip(w, ("wg", "wu", "wd")):
                    m = SP.copy(stream(f"{name}{p % 4}"), part, io[name][i], before, weights_free if p < 4 else None)
                    got.append(m)
                wq[i] = (w, got, users)

            up = Ring([(pair[:, 0:BANK], pair[:, BANK:2 * BANK]) for pair in wide.buffers])
            up.users = [list(wide.users[0]), list(wide.users[1])]
            hidden, rowsof = {}, {}

            split_e, split_d = [], {}

            def split_up(i):
                p = order.index(i)
                while len(split_e) < min(p + 2, EXPERTS):
                    (wg, wu, wd), m_w, users = wq[order[len(split_e)]]
                    split_e.append((split_tile(wg, m_w), split_tile(wu, m_w)))
                    w2, free, users2 = down_ring.take()
                    m = AC.do(lambda e: e.copy(w2[:, 0], wd), m_w, free)
                    m = PO.do(lambda e: e.tensor_tensor(w2[:, 1], wd, w2[:, 0].bitcast(F32), ALU.subtract), m, free)
                    users.append(m)
                    split_d[order[len(split_e) - 1]] = (w2, m, users2)
                return split_e[p]

            def up_half(i, half):
                (bg, bu), free, users = up.take()
                for bank, (w, m_w, w_users) in zip((bg, bu), split_up(i)):
                    m = product(bank, w, half, m_w, m_vT, free)
                    if half == 1:
                        w_users.append(m)
                gate, g_free, g_users = gate_ring.take()
                hid, h_free, h_users = hid_ring.take()
                m_g = AC.do(lambda e: e.activation(gate, bg, ACT.Gelu, bias=gb[:, i:i + 1]), m, m_gb, g_free)
                if i < E:
                    rb, m_rb, rb_users = rowsof[i]
                    m_g = PO.do(lambda e: e.tensor_tensor(gate, gate, rb[:, half * BANK:(half + 1) * BANK], ALU.mult),
                                m_g, m_rb)
                    rb_users.append(m_g)
                m = DV.do(lambda e: e.scalar_tensor_tensor(out=hid, in0=bu, scalar=ub[:, i:i + 1], in1=gate,
                                                           op0=ALU.add, op1=ALU.mult), m, m_g, m_ub, h_free)
                users += [m, m_g]
                g_users.append(m)
                hidden[i, half] = (hid, m, h_users)

            def split_hidden(i, half):
                hid, m, h_users = hidden[i, half]
                hid2, free2, h2_users = hid2_ring.take()
                m = DV.do(lambda e: e.tensor_copy(hid2[:, 0], hid), m, free2)
                m = DV.do(lambda e: e.tensor_tensor(hid2[:, 1], hid, hid2[:, 0].bitcast(F32), ALU.subtract), m, free2)
                h_users.append(m)
                hidden[i, half] = (hid2, m, h2_users)

            def out_cols(c, n=1):
                return psum[:, 4 * BANK + c * D:4 * BANK + (c + n) * D]

            def down_half(i, half):
                w2, m_w, w_users = split_d[i]
                hid2, m_h, h_users = hidden.pop((i, half))
                first = i == order[0]
                for c in range(4 * half, 4 * half + 4):
                    for n, (iw, ih) in enumerate(PRODUCTS):
                        m = PE.do(lambda e: e.matmul(out_cols(c), hid2[:, ih, (c % 4) * P:(c % 4 + 1) * P], w2[:, iw],
                                                     start=(first and c % 2 == 0 and n == 0),
                                                     stop=(i == order[-1] and n == 2), skip_group_check=True),
                                  m_h, m_w, work.users if first else None, mark=(c % 4 == 3 and n == 2))
                h_users.append(m)
                if half == 1:
                    w_users.append(m)
                return m


            def by_chunk(ap):
                return ap.rearrange("p e c -> p c e")

            def over_e(ap):
                return ap.unsqueeze(1).to_broadcast([P, E, NC])

            def first_best(src, best, onehot):
                DV.then(lambda e: e.tensor_reduce(best, by_chunk(src), AX_X, ALU.max))
                DV.then(lambda e: e.tensor_tensor(key, src, over_e(best), ALU.is_equal))
                DV.then(lambda e: e.tensor_tensor(by_chunk(key), by_chunk(key),
                                                  revidx[:, :].unsqueeze(1).to_broadcast([P, NC, E]), ALU.mult), m_rev)
                DV.then(lambda e: e.tensor_reduce(km, by_chunk(key), AX_X, ALU.max))
                DV.then(lambda e: e.tensor_tensor(onehot, key, over_e(km), ALU.is_equal))

            routed = {}

            def router():
                bank, m, users = project_narrow(E, m_narrow, m_vT)
                m = AC.do(lambda e: e.activation(aff, bank[:, 0:NC * E].rearrange("p (c e) -> p e c", c=NC), ACT.Exp,
                                                 scale=-1.0), m)
                users.append(m)
                yield
                DV.do(lambda e: e.tensor_scalar(aff, aff, 1.0, None, ALU.add), m)
                DV.then(lambda e: e.reciprocal(aff, aff))
                first_best(aff, m1, one)
                DV.then(lambda e: e.tensor_tensor(comb, one, over_e(m1), ALU.mult))
                DV.then(lambda e: e.scalar_tensor_tensor(out=aff, in0=one, scalar=-4.0, in1=aff,
                                                         op0=ALU.mult, op1=ALU.add))
                yield
                first_best(aff, m2, one)
                DV.then(lambda e: e.tensor_tensor(c2, one, over_e(m2), ALU.mult))
                DV.then(lambda e: e.tensor_tensor(comb, comb, c2, ALU.add))
                DV.then(lambda e: e.tensor_tensor(den, m1, m2, ALU.add))
                DV.then(lambda e: e.reciprocal(den, den))
                m = DV.then(lambda e: e.tensor_tensor(comb, comb, over_e(den), ALU.mult))
                (bank, _), free, users = up.take()
                m = PE.do(lambda e: e.transpose(bank[:, 0:P], comb.rearrange("p e c -> p (e c)"), ident[:, :]), m, free)
                m = DV.do(lambda e: e.tensor_copy(c2.rearrange("p e c -> p (e c)"), bank[:, 0:P]), m)
                users.append(m)
                routed["scr"] = SP.copy(stream("scratch"), scratch_e[n].rearrange("e (c t) -> (e c) t", c=NC),
                                        c2.rearrange("p e c -> p (e c)"), m)
                routed["rows"] = SP.copy(stream("combT"), combT[0:E, :], scratch_e[n], m_ones_e, routed["scr"])
                yield

            for i in range(4):
                load_expert(i)
            m_v, m_vT = layer_norm(m_in, before, lambda: split_up(order[0]))
            join(m_phase)
            m_wa = SP.copy(stream("wa_e"), wa, io["wa_e"])
            m_gb = SP.copy(stream("gb"), gb, io["gb"])
            m_ub = SP.copy(stream("ub"), ub, io["ub"])
            m_b2 = SP.copy(stream("b2"), b2w[0:EXPERTS, :], io["b2"])
            m_narrow = split_narrow(wa, m_wa, E)
            m_ones_e = DV.do(lambda e: e.memset(combT[0:EXPERTS, :], 1.0))
            router_steps = router()
            steps = [(i, half) for i in order for half in range(2)]
            for s, (i, half) in enumerate(steps):
                for nxt in order[SH:s // 2 + 3] if "scr" in routed else ():
                    if nxt not in rowsof:
                        rowsof[nxt] = load_rows(bcast_ring, scratch_e[n][nxt:nxt + 1, :], routed["scr"])
                up_half(i, half)
                if s == BIAS_AT:
                    m_res = PO.do(lambda e: e.tensor_tensor(x[:, :, :], x[:, :, :], v[:, :, :], ALU.add), m_v)
                    for c in range(NC):
                        PE.do(lambda e, c=c: e.matmul(out_cols(c), combT[0:EXPERTS, c * P:(c + 1) * P],
                                                      b2w[0:EXPERTS, :], start=False, stop=False,
                                                      skip_group_check=True), routed["rows"], m_b2)
                if s >= 2:
                    down_half(*steps[s - 2])
                split_hidden(i, half)
                next(router_steps, None)
                if s >= 3 and s % 2 == 1 and s // 2 + 3 < len(order):
                    load_expert(s // 2 + 3)
            m_last = [down_half(*s) for s in steps[-2:]]
            m_out = []
            for q in range(4):
                m = DV.do(lambda e, q=q: e.tensor_tensor(
                    x[:, 2 * q:2 * q + 2, :], out_cols(2 * q, 2).rearrange("p (c d) -> p c d", c=2),
                    x[:, 2 * q:2 * q + 2, :], ALU.add), m_last[q // 2], m_res)
                m_out += [m, m]
            return m_out, [PE.last(), m_res], G.at


        m_x1, v_free, experts_end = experts(0, m_xa, v_free, weights_free)

        m_phase = queued()
        B = Arena()
        Bt, Ct, Bs = (B(T) for _ in range(3))
        ud_ring = Ring([B(WB) for _ in range(2)])
        U = B(NC * WB).rearrange("p (c m) -> p c m", c=NC)
        assert B.at >= experts_end
        w_ring = Ring([B(KD * P).rearrange("p (k m) -> p k m", k=KD) for _ in range(3)])
        cw = B(6 * TAPS).rearrange("p (i k) -> p i k", k=TAPS)
        cb, nw = B(6), B(XT)
        wdt = B(KD * HB).rearrange("p (k h) -> p k h", k=KD)
        dtb, alog, dskip = B(HB), B(HB), B(HB)
        xt = B(XT * T).rearrange("p (i t) -> p i t", i=XT)
        padded = xt.rearrange("p i t -> p (i t)")
        u_padded = padded.rearrange("p (c j s w) -> p c j s w", c=NC, j=4, s=SUBS)
        zc = B(XT * T).rearrange("p (i t) -> p i t", i=XT)
        G, intra = B(T), B(T)
        y = B(NC * WB).rearrange("p (c m) -> p c m", c=NC)
        st_ring = Ring([B(WB) for _ in range(2)])
        wout = B(XT * D).rearrange("p (i d) -> p i d", i=XT)
        ssq, rms = B(NC), B(NC)
        minus = B(HB * NC)
        small_b = B(13 * HB * NC).rearrange("p (i n) -> p i n", i=13)
        raw_b = y.rearrange("p c m -> p (c m)")[:, 0:HB * NC]

        loaded_b = []

        def load_tile_b():
            n = len(loaded_b)
            if n < 6 + XT:
                w, before, users = w_ring.take()
                loaded_b.append((w, SP.copy(stream(f"wb{n % 3}"), w, io["w_b"][n], before), users))

        for _ in w_ring.buffers:
            load_tile_b()
        m_cw = SP.copy(stream("cw"), cw, io["conv_b"])
        m_cb = SP.copy(stream("cb"), cb, io["convbias_b"])
        m_nw = SP.copy(stream("nw"), nw, io["norm_b"])
        m_wdt = SP.copy(stream("wdt"), wdt, io["wdt_b"])
        m_dtb = SP.copy(stream("dtb"), dtb, io["dtb_b"].to_broadcast([P, HB]))
        m_alog = SP.copy(stream("alog"), alog, io["alog_b"].to_broadcast([P, HB]))
        m_dsk = SP.copy(stream("dskip"), dskip, io["d_b"].to_broadcast([P, HB]))
        m_wout = SP.copy(stream("wo"), wout, io["wout_b"])
        split_b = []

        def split_tile_b(ahead):
            while len(split_b) < min(ahead, 6 + XT):
                w, m_w, users = loaded_b[len(split_b)]
                split_b.append(split_tile(w, m_w))
                users.append(split_b[-1][1])
                load_tile_b()

        m_cw = DV.do(lambda e: e.tensor_scalar(cw, cw, 0.5, None, ALU.mult), m_cw)
        _, m_vT = layer_norm(m_x1, v_free, lambda: split_tile_b(4))
        join(m_phase)

        def project_b(i):
            split_tile_b(i + SPLITS - 1)
            return project(*split_b[i], m_vT)

        fb, m_cv, m_z = {}, [], []
        term_ring = Ring([intra])
        by_turn = [16 * i + SUBS * j + s for i in range(XT) for s in range(SUBS) for j in range(4)]
        rows = {}
        spare = [v[:, i * 4:(i + 1) * 4, :].rearrange("p c d -> p (c d)") for i in range(2)] + [B(T)]
        spare += [small_b[:, 2 * i:2 * i + 2, :].rearrange("p i n -> p (i n)") for i in range(3)]
        bt_read, factors_there = [], []
        rows_ring = Ring(list(enumerate(bcast + spare + [Bt])))
        EARLY = len(bcast) + 2
        SHARE = {"pool": 5, "act": 4}
        OF = 16

        def engine_of(n):
            if n < EARLY:
                return "pool"
            if (n + 1) * SHARE["pool"] // OF > n * SHARE["pool"] // OF:
                return "pool"
            free = OF - SHARE["pool"]
            k = n - (n + 1) * SHARE["pool"] // OF
            return "act" if (k + 1) * SHARE["act"] // free > k * SHARE["act"] // free else "dve"

        def load_head(n):
            rows[n] = load_rows(rows_ring, scratch_b[by_turn[n]:by_turn[n] + 1, :], fb["rows"])

        def exponents(n):
            buf, m, users = rows[n]
            h = by_turn[n]
            cum = fb["cumhi"][:, h * NC:(h + 1) * NC]
            r3 = buf.rearrange("p (c t) -> p c t", t=P)
            if engine_of(n) == "pool":
                m = PO.do(lambda e: e.tensor_tensor(r3, r3, spread(cum, P), ALU.subtract), m, fb["cum_there"])
            if engine_of(n) in ("pool", "act"):
                m = PO.do(lambda e: e.affine_select(out=r3, in_=r3, compare_op=ALU.is_ge, fill=MASKED, base=0,
                                                    pattern=[[0, NC], [1, P]], channel_multiplier=-1), m)
            else:
                for c in range(NC):
                    m = DV.do(lambda e: e.tensor_scalar(r3[:, c, :], r3[:, c, :], cum[:, c:c + 1], 0.0,
                                                        ALU.subtract, ALU.min), m, fb["cum_there"], mark=(c == NC - 1))
            rows[n] = (buf, m, users)

        def decay_head(n):
            buf, m, users = rows[n]
            if engine_of(n) == "act":
                for c in range(NC):
                    b = chunk(buf, c)
                    bias = fb["minus"][:, by_turn[n] * NC + c:by_turn[n] * NC + c + 1]
                    m = AC.do(lambda e: e.activation(b, b, ACT.Exp, bias=bias), m, fb["minus_there"], mark=(c == NC - 1))
            else:
                m = AC.do(lambda e: e.activation(buf, buf, ACT.Exp), m)
            rows[n] = (buf, m, users)

        def project_all():
            convolved = [Bt, Ct] + [xt[:, q, :] for q in range(XT)]
            for i, dst in enumerate(convolved):
                if i >= 2:
                    bank, m, users = project_b(2 + 2 * (i - 2))
                    late_silu()
                    m_z.append(AC.do(lambda e: e.activation(zc[:, i - 2, :], bank, ACT.Silu, scale=0.25), m))
                    users.append(m_z[-1])
                    yield
                bank, m, users = project_b(i if i < 2 else 3 + 2 * (i - 2))
                yield from conv(dst, bank, m, cw[:, i, :], [m_cw, m_cb], None, users, m_cv, bias=cb[:, i:i + 1],
                                spare=term_ring if i in (1, 2, 3) else None)
                yield
            late_silu()

        def factors_b():
            m_raw = project_dt(wdt, m_wdt, HB, dtb, m_dtb, raw_b)
            yield
            n = -WAIT_ROWS
            for _ in decays(fb, HB, raw_b, m_raw, alog, m_alog, scratch_b, small_b, dskip, m_dsk):
                if "rows" in fb:
                    if n == -WAIT_ROWS:
                        fb["minus"] = minus
                        fb["minus_there"] = DV.do(lambda e: e.tensor_scalar(minus, fb["cumhi"], -1.0, None, ALU.mult),
                                                  fb["cum_there"])
                        rows_ring.users = bcast_ring.users + [[m_vT] for _ in range(3)]
                        rows_ring.users += [[factors_there] for _ in range(3)] + [bt_read]
                    for h in range(len(rows), min(2 * (n + WAIT_ROWS) + 2, EARLY)):
                        load_head(h)
                    if 0 <= n < EARLY:
                        exponents(n)
                    if 0 < n <= EARLY:
                        decay_head(n - 1)
                    n += 1
                yield
            factors_there.append(fb["marks"])
            for n in range(n, EARLY + 1):
                if n < EARLY:
                    exponents(n)
                if n > 0:
                    decay_head(n - 1)
                yield

        tiles = project_all()
        next(tiles)
        interleave(factors_b(), DECAY_STEPS + 2, tiles, 5 * 6 - 3 + XT)
        m_fb = fb["marks"]

        m_bs, m_g, m_u = [], [], []
        for q in range(2):
            bank, free, users = work.take()
            for c in range(4 * q, 4 * q + 4):
                m = PE.do(lambda e, c=c, bank=bank: e.transpose(bank[:, (c % 4) * P:(c % 4 + 1) * P],
                                                                Bt[:, c * P:(c + 1) * P], ident[:, :]), m_cv[0], free)
            m = AC.do(lambda e, q=q, bank=bank: e.copy(Bs[:, q * BANK:(q + 1) * BANK], bank), m)
            users.append(m)
            m_bs.append(m)
            bank, free, users = work.take()
            for c in range(4 * q, 4 * q + 4):
                m = PE.do(lambda e, c=c, bank=bank: e.matmul(bank[:, (c % 4) * P:(c % 4 + 1) * P],
                                                             Bt[:, c * P:(c + 1) * P], Ct[:, c * P:(c + 1) * P],
                                                             start=True, stop=True), m_cv[0:2], free)
            m = AC.do(lambda e, q=q, bank=bank: e.copy(G[:, q * BANK:(q + 1) * BANK], bank), m)
            users.append(m)
            m_g.append(m)

        bt_read += [m_bs, m_g]
        g3 = G.rearrange("p (c t) -> p c t", t=P)
        m_g = PO.do(lambda e: e.affine_select(out=g3, in_=g3, compare_op=ALU.is_ge, fill=0.0, base=0,
                                              pattern=[[0, NC], [1, P]], channel_multiplier=-1), m_g)

        def per_head(name, c):
            return spread(fb[name].rearrange("p (h c) -> p h c", c=NC)[:, :, c], PB)

        def heads(ap):
            return ap.rearrange("p (h m) -> p h m", m=PB)

        m_y0 = []

        def token_major(c):
            bank, free, users = work.take()
            for i in range(XT):
                m_t = PE.do(lambda e: e.transpose(bank[:, i * P:(i + 1) * P], chunk(xt[:, i, :], c), ident[:, :]),
                            m_cv[2 + i], free)
            for dst, name, marks in ((U, "dtl", m_u), (y, "skip", m_y0)):
                marks.append(DV.do(lambda e: e.tensor_tensor(heads(dst[:, c, :]), heads(bank), per_head(name, c),
                                                             ALU.mult), m_t, m_fb))
            users.append(m_y0[-1])

        for c in range(NC):
            token_major(c)

        m_y = [m_y0[0]]
        part_ring = Ring([intra[:, i * WB:(i + 1) * WB] for i in range(2)])
        part_ring.users = [[term_ring.users] for _ in range(2)]
        def states_b():
            added, given = None, None
            st = old = m_st = st_users = old_users = None

            def scaled(c):
                ud, ud_free, ud_users = ud_ring.take()
                return ud, PO.do(lambda e: e.tensor_tensor(heads(ud), heads(U[:, c, :]), per_head("wd", c), ALU.mult),
                                 m_u[c], m_fb, ud_free), ud_users

            ud = scaled(0)
            yield
            for c in range(NC + 1):
                if added is not None:
                    bank, m_s, b_users = added
                    old, old_users = st, st_users
                    st, st_free, st_users = st_ring.take()
                    if c == 1:
                        m_st = DV.do(lambda e: e.tensor_copy(st, bank), m_s, st_free)
                    else:
                        md = DV.do(lambda e: e.tensor_tensor(heads(st), heads(old), per_head("dec", c - 1), ALU.mult),
                                   m_st, st_free, m_fb)
                        m_st = DV.do(lambda e: e.tensor_tensor(st, bank, st, ALU.add), m_s, md)
                        old_users.append(md)
                    b_users.append(m_st)
                if given is not None:
                    bank, m_g, b_users = given
                    part, p_free, p_users = part_ring.take()
                    m = DV.do(lambda e: e.tensor_tensor(heads(part), heads(bank), per_head("ehi", c - 1), ALU.mult),
                              m_g, m_fb, p_free)
                    b_users.append(m)
                    m = PO.do(lambda e: e.tensor_tensor(y[:, c - 1, :], y[:, c - 1, :], part, ALU.add), m, m_y0[c - 1])
                    p_users.append(m)
                    m_y.append(m)
                given = None
                if added is not None:
                    bank, free, users = work.take()
                    m = PE.do(lambda e: e.matmul(bank, chunk(Ct, c), st, start=True, stop=True), m_st, m_cv[1], free)
                    st_users.append(m)
                    given = bank, m, users
                added = None
                if c < NC - 1:
                    u, m, ud_users = ud
                    bank, free, users = work.take()
                    m = PE.do(lambda e: e.matmul(bank, chunk(Bs, c), u, start=True, stop=True), m, m_bs, free)
                    ud_users.append(m)
                    added = bank, m, users
                    if c + 1 < NC - 1:
                        ud = scaled(c + 1)
                yield

        states = states_b()
        next(states)
        m_pad = PO.do(lambda e: e.memset(padded, 0.0), m_u)
        next(states)
        loaded = EARLY
        m_yb = []
        pad_users, intra_users = [], []

        def pad(i):
            cs = slice(i * P, (i + 1) * P)
            src = U[:, :, cs].rearrange("p c (j s m) -> p c j s m", j=4, m=PB)
            for s in range(SUBS):
                m = AC.do(lambda e: e.copy(u_padded[:, :, :, s, s * PB:(s + 1) * PB], src[:, :, :, s, :]),
                          m_pad, m_u, pad_users)
            return m

        def finish_tile(i, pair, m, users):
            m = AC.do(lambda e: e.copy(intra, pair), m, intra_users, m_y)
            users.append(m)
            ws = slice(i * P, (i + 1) * P)
            for q in range(2):
                cs = slice(4 * q, 4 * q + 4)
                m_t = unit(transposes(lambda c: chunk(intra, 4 * q + c)), 4, [m, m_ident],
                           lambda bank, m: DV.do(lambda e: e.tensor_tensor(
                               y[:, cs, ws], bank.rearrange("p (c m) -> p c m", c=4), y[:, cs, ws], ALU.add), m, m_y))
            intra_users[:] = [PE.last()]
            for q in range(2):
                cs = slice(4 * q, 4 * q + 4)
                elo = fb["elo"].rearrange("p (h c) -> p c h", c=NC)[:, cs, 16 * i:16 * (i + 1)]
                y4 = y[:, cs, ws].rearrange("p c (h m) -> p c h m", m=PB)
                m = PO.do(lambda e: e.tensor_tensor(y4, y4, spread(elo, PB), ALU.mult), m_t)
            m_yb.append(m)

        LEAD = 4
        GROW_AT = len(rows_ring.buffers)
        late = None
        for n, h in enumerate(by_turn):
            i, s, j = n // 16, n // 4 % SUBS, n % 4
            if n % 16 == 0:
                m_up = pad(i)
                pair, free, p_users = wide.take()
                batch = []
            while loaded < min(n + len(rows_ring.buffers) - 3, HB):
                load_head(loaded)
                loaded += 1
                if loaded == 2 * GROW_AT:
                    rows_ring.grow([(GROW_AT, Ct), (GROW_AT + 1, Bs)], [m_y, PE.last()])
            if EARLY <= n + LEAD < HB:
                exponents(n + LEAD)
            if EARLY <= n + LEAD - 1 < HB:
                decay_head(n + LEAD - 1)
            buf, m, users = rows.pop(n)
            m = DV.do(lambda e: e.tensor_tensor(buf, buf, G, ALU.mult), m, m_g)
            batch.append((buf, m, users))
            if j == 3:
                for c in range(NC):
                    for jj, (buf, m, _) in enumerate(batch):
                        m = PE.do(lambda e: e.matmul(pair[jj * QUAD:(jj + 1) * QUAD, c * P:(c + 1) * P],
                                                     u_padded[:, c, jj, s, :], chunk(buf, c), start=(s == 0 and c % 4 == 0),
                                                     stop=(s == SUBS - 1), skip_group_check=True),
                                  m, m_up, free, mark=(c == NC - 1 and jj == 3))
                for _, _, users in batch:
                    users.append(m)
                batch = []
            next(states, None)
            if n % 16 == 6 and late is not None:
                finish_tile(*late)
                late = None
            if n % 16 == 15:
                pad_users[:] = [m]
                late = (i, pair, m, p_users)
        m_early_free = PE.last()
        finish_tile(*late)
        bcast_ring.users = rows_ring.users[:len(bcast)]
        m_rows_free = rows_ring.users
        for c in range(NC):
            m = AC.do(lambda e, c=c: e.activation(U[:, c, :], y[:, c, :], ACT.Square, accum_out=ssq[:, c:c + 1]),
                      m_yb, PE.last())
        m = PO.do(lambda e: e.tensor_scalar(rms, ssq, 1.0 / WB, None, ALU.mult), m)
        m = PO.do(lambda e: e.tensor_scalar(rms, rms, 1e-5, None, ALU.add), m)
        m_rms = PO.do(lambda e: e.tensor_tensor(rms, rms, neghalf[:, 0:NC], ALU.pow), m)
        m_gt = []
        m_x2 = []
        for q in range(2):
            for i in range(XT):
                bank, free, users = work.take()
                for c in range(4 * q, 4 * q + 4):
                    m = PE.do(lambda e, c=c, i=i, bank=bank: e.transpose(bank[:, (c % 4) * P:(c % 4 + 1) * P],
                                                                         y[:, c, i * P:(i + 1) * P], ident[:, :]),
                              m_yb, free)
                ts = slice(q * BANK, (q + 1) * BANK)
                m = DV.do(lambda e, i=i, ts=ts, bank=bank: e.scalar_tensor_tensor(
                    out=xt[:, i, ts], in0=bank, scalar=nw[:, i:i + 1], in1=zc[:, i, ts], op0=ALU.mult, op1=ALU.mult),
                    m, m_z, m_nw, m_rows_free)
                users.append(m)
                m_gt.append(m)
            for c2 in (4 * q, 4 * q + 2):
                bank, free, users = work.take()
                for c in (c2, c2 + 1):
                    for i in range(XT):
                        m = PE.do(lambda e, c=c, i=i, bank=bank: e.matmul(
                            bank[:, (c % 2) * D:(c % 2 + 1) * D], xt[:, i, c * P:(c + 1) * P], wout[:, i, :],
                            start=(i == 0), stop=(i == XT - 1)), m_gt, m_wout, free)
                for c in (c2, c2 + 1):
                    m_c = DV.do(lambda e, c=c, bank=bank: e.scalar_tensor_tensor(
                        out=x[:, c, :], in0=bank[:, (c % 2) * D:(c % 2 + 1) * D], scalar=rms[:, c:c + 1],
                        in1=x[:, c, :], op0=ALU.mult, op1=ALU.add), m, m_rms)
                    m_x2.append(m_c)
                users.append(m_c)
        m_x3, _, _ = experts(1, m_x2, [PE.last(), m_rows_free], m_early_free)
        m_out = [SP.copy(stream(f"x{c}"), io["out"][c * P:(c + 1) * P, :], x[:, c, :], m_x3[c]) for c in range(NC)]
        SP.wait(m_out)


def kernel(**inputs):
    import concourse.bacc as bacc
    from concourse.bass_utils import run_bass_kernel_spmd

    a = {n: np.ascontiguousarray(np.asarray(t)) for n, t in inputs.items()}

    def k_major(w):
        return w.reshape(KD, P, -1).transpose(1, 0, 2)

    win = a["L0_attn_a_Win"]
    wx, wz = win[:HA * PA], win[HA * PA:2 * HA * PA]
    wb, wc = (win[2 * HA * PA + i * HA * NS:2 * HA * PA + (i + 1) * HA * NS].reshape(PAIRS, 2, NS, D) for i in range(2))
    w_a = np.stack([wx.reshape(PAIRS, P, D), wb[:, 0], wb[:, 1], wc[:, 0], wc[:, 1], wz.reshape(PAIRS, P, D)], 1)
    w_a = w_a.reshape(PAIRS, 6, P, KD, P).transpose(0, 4, 3, 1, 2)
    cb_, cc_ = (a[f"L0_attn_a_conv_w_{n}"].reshape(PAIRS, 2, NS, TAPS) for n in "bc")
    cx_ = a["L0_attn_a_conv_w_x"].reshape(PAIRS, P, TAPS)
    conv_a = np.stack([cx_, cb_[:, 0], cb_[:, 1], cc_[:, 0], cc_[:, 1]], 1).transpose(2, 0, 1, 3)
    wib = a["L0_attn_b_in_proj_w"]
    order = [wib[:, 2 * WB:2 * WB + NS], wib[:, 2 * WB + NS:2 * WB + 2 * NS]]
    order += [wib[:, off + i * P:off + (i + 1) * P] for i in range(XT) for off in (0, WB)]
    cwb, cbb = a["L0_attn_b_conv_w"], a["L0_attn_b_conv_b"]
    tiles_b = [slice(WB, WB + NS), slice(WB + NS, WB + 2 * NS)] + [slice(i * P, (i + 1) * P) for i in range(XT)]
    f = {n: a[f"L0_ffn_{n}"] for n in ("wa", "rg", "rgb", "rw1", "rb1", "rw2", "rb2", "sg", "sgb", "sw1", "sb1",
                                       "sw2", "sb2")}

    def up(routed, shared):
        return np.concatenate([routed, shared]).reshape(EXPERTS, KD, P, F).transpose(0, 2, 1, 3)

    arrays = {
        "x": a["L0_attn_a_x"].reshape(T, D),
        "w_a": w_a,
        "wdt_a": k_major(win[-HA:].T),
        "conv_a": conv_a,
        "dtb_a": a["L0_attn_a_dt_bias"].reshape(1, HA),
        "alog_a": a["L0_attn_a_A_log"].reshape(1, HA),
        "wout_a": a["L0_attn_a_Wout"].T.reshape(PAIRS // GROUP, GROUP, P, D).transpose(0, 2, 1, 3),
        "w_b": np.stack([k_major(w) for w in order]),
        "wdt_b": k_major(wib[:, -HB:]),
        "conv_b": np.stack([cwb[s] for s in tiles_b], 1),
        "convbias_b": np.stack([cbb[s] for s in tiles_b], 1),
        "norm_b": a["L0_attn_b_norm_w"].reshape(XT, P).T,
        "dtb_b": a["L0_attn_b_dt_bias"].reshape(1, HB),
        "alog_b": a["L0_attn_b_A_log"].reshape(1, HB),
        "d_b": a["L0_attn_b_D"].reshape(1, HB),
        "wout_b": a["L0_attn_b_out_proj_w"].reshape(XT, P, D).transpose(1, 0, 2),
        "wa_e": k_major(f["wa"]),
        "wg": up(f["rg"], f["sg"]),
        "wu": up(f["rw1"], f["sw1"]),
        "wd": np.concatenate([f["rw2"], f["sw2"]]),
        "gb": np.concatenate([f["rgb"], f["sgb"]]).T,
        "ub": np.concatenate([f["rb1"], f["sb1"]]).T,
        "b2": np.concatenate([f["rb2"], f["sb2"]]),
        "ident": np.eye(P, dtype=np.float32),
        "tri": np.triu(np.ones((P, P), np.float32)),
        "revidx": (E - np.arange(E, dtype=np.float32)).reshape(1, E),
    }
    arrays = {n: np.ascontiguousarray(t) for n, t in arrays.items()}
    nc = bacc.Bacc("TRN2", target_bir_lowering=False, num_devices=1)
    io = {n: nc.dram_tensor(f"in_{n}", t.shape, F32, kind="ExternalInput").ap() for n, t in arrays.items()}
    io["out"] = nc.dram_tensor("out", (T, D), F32, kind="ExternalOutput").ap()
    hybrid_block(nc, io)
    r = run_bass_kernel_spmd(nc, [{f"in_{n}": t for n, t in arrays.items()}], core_ids=[0])
    return r.results[0]["out"].reshape(1, T, D)
```
